# Optimizing a Trainium2 kernel written in Bass

```python
import numpy as np
import jax
import jax.numpy as jnp

def _softmax(x, axis=-1):
    return jax.nn.softmax(x, axis=axis)

def _gelu(x):
    return jax.nn.gelu(x, approximate=True)

def _silu(x):
    return jax.nn.silu(x)

def _sigmoid(x):
    return jax.nn.sigmoid(x)

def _layernorm(x, axis=-1, eps=1e-05):
    m = jnp.mean(x, axis=axis, keepdims=True)
    v = jnp.var(x, axis=axis, keepdims=True)
    return (x - m) / jnp.sqrt(v + eps)

def _scatter_add(tgt, idx, src, axis=0):
    return tgt.at[idx].add(src)

def _segment_sum(src, seg, n):
    return jax.ops.segment_sum(src, seg, n)
kernel_name = 'mk_macaron_d1_jaxref_r4_d1dc18'

def setup_inputs(seed: int=0):
    np.random.seed(seed)
    _w = jnp.asarray

    def _L0_attn_setup():
        import jax, jax.numpy as jnp
        import numpy as np
        import math
        NHEAD = 16
        FACTOR = 5
        key = jax.random.key(seed)
        ks = jax.random.split(key, 10)
        B, L, Dm = (2, 512, 256)
        x = jax.random.normal(ks[0], (B, L, Dm), dtype=jnp.float32)
        w = lambda k: jax.random.normal(k, (Dm, Dm), dtype=jnp.float32) * 0.02
        b = lambda k: jax.random.normal(k, (Dm,), dtype=jnp.float32) * 0.02
        return {'x': x, 'Wq': w(ks[1]), 'bq': b(ks[2]), 'Wk': w(ks[3]), 'bk': b(ks[4]), 'Wv': w(ks[5]), 'bv': b(ks[6]), 'Wo': w(ks[7]), 'bo': b(ks[8])}
    _L0_attn_in = _L0_attn_setup()

    def _L0_ffn_setup():
        import jax, jax.numpy as jnp
        import numpy as np
        HIDDEN = 256
        HEAD_DIM = 64
        N_EXPERTS = 16
        MIN_EXPERTS = 2
        B, T = (4, 512)

        def _normalize(x, axis):
            n = jnp.sqrt(jnp.sum(x * x, axis=axis, keepdims=True))
            return x / jnp.maximum(n, 1e-12)

        def _ste(x):
            hard = jax.lax.stop_gradient((x > 0).astype(x.dtype))
            return hard + x - jax.lax.stop_gradient(x)

        def _gating(hidden_states, sim_matrix, gates):
            b, t, c = hidden_states.shape
            flat = hidden_states.reshape(b * t, c)
            logits = _normalize(flat, -1) @ _normalize(sim_matrix, 0) - jax.nn.sigmoid(gates)
            gated = jax.nn.relu(logits)
            mask = _ste(gated)
            inactive = jnp.sum(mask, axis=1) == 0
            _, fb_idx = jax.lax.top_k(logits, MIN_EXPERTS)
            fb = jnp.zeros_like(mask).at[jnp.arange(b * t)[:, None], fb_idx].set(1.0)
            fb_applied = inactive[:, None] & (fb > 0)
            mask = jnp.where(fb_applied, 1.0, mask)
            masked_logits = jnp.where(mask > 0, gated, -jnp.inf)
            return jax.nn.softmax(masked_logits, axis=-1).reshape(b, t, -1)
        key = jax.random.key(seed)
        ks = jax.random.split(key, 6)
        xav_qkv = float(np.sqrt(6.0 / (HIDDEN + HEAD_DIM)))
        return {'hidden_states': jax.random.normal(ks[0], (B, T, HIDDEN), dtype=jnp.float32), 'sim_matrix': jax.random.normal(ks[1], (HIDDEN, N_EXPERTS), dtype=jnp.float32), 'gates': jnp.zeros((N_EXPERTS,), dtype=jnp.float32), 'q_proj': jax.random.uniform(ks[2], (N_EXPERTS, HIDDEN, HEAD_DIM), jnp.float32, -xav_qkv, xav_qkv), 'k_proj': jax.random.uniform(ks[3], (N_EXPERTS, HIDDEN, HEAD_DIM), jnp.float32, -xav_qkv, xav_qkv), 'v_proj': jax.random.uniform(ks[4], (N_EXPERTS, HIDDEN, HEAD_DIM), jnp.float32, -xav_qkv, xav_qkv), 'o_proj': jax.random.uniform(ks[5], (N_EXPERTS, HEAD_DIM, HIDDEN), jnp.float32, -xav_qkv, xav_qkv)}
    _L0_ffn_in = _L0_ffn_setup()
    _d = {'L0_attn_x': _L0_attn_in['x'], 'L0_attn_Wq': _L0_attn_in['Wq'], 'L0_attn_bq': _L0_attn_in['bq'], 'L0_attn_Wk': _L0_attn_in['Wk'], 'L0_attn_bk': _L0_attn_in['bk'], 'L0_attn_Wv': _L0_attn_in['Wv'], 'L0_attn_bv': _L0_attn_in['bv'], 'L0_attn_Wo': _L0_attn_in['Wo'], 'L0_attn_bo': _L0_attn_in['bo'], 'L0_ffn_sim_matrix': _L0_ffn_in['sim_matrix'], 'L0_ffn_gates': _L0_ffn_in['gates'], 'L0_ffn_q_proj': _L0_ffn_in['q_proj'], 'L0_ffn_k_proj': _L0_ffn_in['k_proj'], 'L0_ffn_v_proj': _L0_ffn_in['v_proj'], 'L0_ffn_o_proj': _L0_ffn_in['o_proj']}
    _x0 = _d['L0_attn_x']
    _d['L0_attn_x'] = jax.random.normal(jax.random.fold_in(jax.random.key(seed), 1), (16, 512, 256), dtype=_x0.dtype)
    del _x0
    return _d

def reference(L0_attn_x, L0_attn_Wq, L0_attn_bq, L0_attn_Wk, L0_attn_bk, L0_attn_Wv, L0_attn_bv, L0_attn_Wo, L0_attn_bo, L0_ffn_sim_matrix, L0_ffn_gates, L0_ffn_q_proj, L0_ffn_k_proj, L0_ffn_v_proj, L0_ffn_o_proj):

    def _L0_attn_ref(x, Wq, bq, Wk, bk, Wv, bv, Wo, bo):
        import jax, jax.numpy as jnp
        import numpy as np
        import math
        NHEAD = 16
        FACTOR = 5
        B, L, Dm = x.shape
        H = NHEAD
        D = Dm // H
        U = min(L, int(FACTOR * math.log(L)) if L > 1 else L)

        def proj(W, b):
            return (x @ W.T + b).reshape(B, L, H, D).transpose(0, 2, 1, 3)
        Q = proj(Wq, bq)
        K = proj(Wk, bk)
        V = proj(Wv, bv)
        scores = jnp.einsum('bhqd,bhkd->bhqk', Q, K) / math.sqrt(D)
        thresh = jax.lax.top_k(scores, U)[0][..., -1:]
        scores = jnp.where(scores < thresh, -jnp.inf, scores)
        attn = jax.nn.softmax(scores, axis=-1)
        context = jnp.einsum('bhqk,bhkd->bhqd', attn, V)
        context = context.transpose(0, 2, 1, 3).reshape(B, L, Dm)
        return context @ Wo.T + bo

    def _L0_ffn_ref(hidden_states, sim_matrix, gates, q_proj, k_proj, v_proj, o_proj):
        import jax, jax.numpy as jnp
        import numpy as np
        HIDDEN = 256
        HEAD_DIM = 64
        N_EXPERTS = 16
        MIN_EXPERTS = 2
        B, T = (4, 512)

        def _normalize(x, axis):
            n = jnp.sqrt(jnp.sum(x * x, axis=axis, keepdims=True))
            return x / jnp.maximum(n, 1e-12)

        def _ste(x):
            hard = jax.lax.stop_gradient((x > 0).astype(x.dtype))
            return hard + x - jax.lax.stop_gradient(x)

        def _gating(hidden_states, sim_matrix, gates):
            b, t, c = hidden_states.shape
            flat = hidden_states.reshape(b * t, c)
            logits = _normalize(flat, -1) @ _normalize(sim_matrix, 0) - jax.nn.sigmoid(gates)
            gated = jax.nn.relu(logits)
            mask = _ste(gated)
            inactive = jnp.sum(mask, axis=1) == 0
            _, fb_idx = jax.lax.top_k(logits, MIN_EXPERTS)
            fb = jnp.zeros_like(mask).at[jnp.arange(b * t)[:, None], fb_idx].set(1.0)
            fb_applied = inactive[:, None] & (fb > 0)
            mask = jnp.where(fb_applied, 1.0, mask)
            masked_logits = jnp.where(mask > 0, gated, -jnp.inf)
            return jax.nn.softmax(masked_logits, axis=-1).reshape(b, t, -1)
        b, t, c = hidden_states.shape
        rw = _gating(hidden_states, sim_matrix, gates)
        q = jnp.einsum('bte,bted->btd', rw, jnp.einsum('btc,ecd->bted', hidden_states, q_proj))
        k = jnp.einsum('bte,bted->btd', rw, jnp.einsum('btc,ecd->bted', hidden_states, k_proj))
        v = jnp.einsum('bte,bted->btd', rw, jnp.einsum('btc,ecd->bted', hidden_states, v_proj))
        scale = 1.0 / jnp.sqrt(jnp.asarray(HEAD_DIM, dtype=q.dtype))
        scores = jnp.einsum('bqd,bkd->bqk', q, k) * scale
        causal = jnp.tril(jnp.ones((t, t), dtype=bool))
        scores = jnp.where(causal, scores, -jnp.inf)
        attn = jnp.einsum('bqk,bkd->bqd', jax.nn.softmax(scores, axis=-1), v)
        mixed = attn[:, :, None, :] * rw[..., None]
        return jnp.einsum('bted,edc->btc', mixed, o_proj)
    x = L0_attn_x
    x = x + 0.5 * _L0_ffn_ref(_layernorm(x, axis=-1), L0_ffn_sim_matrix, L0_ffn_gates, L0_ffn_q_proj, L0_ffn_k_proj, L0_ffn_v_proj, L0_ffn_o_proj)
    x = x + _L0_attn_ref(_layernorm(x, axis=-1), L0_attn_Wq, L0_attn_bq, L0_attn_Wk, L0_attn_bk, L0_attn_Wv, L0_attn_bv, L0_attn_Wo, L0_attn_bo)
    x = x + 0.5 * _L0_ffn_ref(_layernorm(x, axis=-1), L0_ffn_sim_matrix, L0_ffn_gates, L0_ffn_q_proj, L0_ffn_k_proj, L0_ffn_v_proj, L0_ffn_o_proj)
    return x

_drawn_inputs = setup_inputs


def setup_inputs(seed=0):
    import zlib

    import numpy as np

    out = dict(_drawn_inputs(seed))
    spreads = {'L0_ffn_gates': (0.0, 0.1)}
    factors = {'L0_attn_bq': 8.0, 'L0_attn_bk': 8.0, 'L0_attn_bv': 7.54, 'L0_attn_bo': 2.779}
    for name, (base, spread) in spreads.items():
        noise = np.random.default_rng([zlib.crc32(name.encode()), seed]).standard_normal(out[name].shape)
        drawn = base * np.exp(spread * noise) if base else spread * noise
        out[name] = jnp.asarray(drawn.astype(out[name].dtype))
    for name, factor in factors.items():
        out[name] = (out[name] * factor).astype(out[name].dtype)
    return out
```

```python
from contextlib import ExitStack

import concourse.bass as bass
from concourse import mybir

F32 = mybir.dt.float32
ALU = mybir.AluOpType
ACT = mybir.ActivationFunctionType
ds = bass.ds

P = 128
NB, T, D = 16, 512, 256
KC = D // P
TPB = T // P
TILES = NB * TPB
H, HD = 16, D // 16
HG = 4
GROUPS = H // HG
STEPS = NB * GROUPS
UNITS = HG * TPB
E, ED = 16, 64
QKV = 3 * ED
TOPK = 31
ROUNDS = (TOPK + 7) // 8
LAST = TOPK - 8 * (ROUNDS - 1) - 1
SLOTS = 16
RING = 8
TOP_LAG, EXP_LAG, OUT_LAG, CTX_LAG = 3, 4, 5, 6
LAG_B = 5
LAG_A = 5
RINGX = 12
CHUNKS = E // 2
CTXW = HG * (HD + 1)
BIG = 3.0e38
MASKED = -1.0e37
START = {"a": 2, "b": 0}


def build(nc, x, wqk, bqk, wv, bv, wo, bo, sim, gates, wf, wof, out):
    with ExitStack() as ctx:
        def sb(name, *shape):
            return ctx.enter_context(nc.sbuf_tensor(name, list(shape), F32))

        def bank(name):
            return ctx.enter_context(nc.psum_tensor(name, [P, 512], F32))

        def sem(name):
            return ctx.enter_context(nc.semaphore(name))

        ident = sb("ident", P, P)
        ones = sb("ones", P, P)
        minus_half = sb("minus_half", P, E)
        minus_one = sb("minus_one", P, 1)
        simg = sb("simg", P, E)
        maskw = sb("maskw", P, (2 * TPB - 1) * P)
        wo_sb = sb("wo_sb", P, KC, D)
        bo_row = sb("bo_row", 1, D)
        wf_sb = sb("wf_sb", P, KC, E * QKV)
        wof_sb = sb("wof_sb", P, E * ED // P, D)
        simn = sb("simn", P, KC, E)
        simsq = sb("simsq", P, KC, E)
        simr = sb("simr", P, E)
        gate_row = sb("gate_row", 1, 4, E)
        sig = sb("sig", P, E)

        wqk_cur = sb("wqk_cur", P, 2 * KC, P)
        bqk_cur = sb("bqk_cur", P, 2)
        wv_cur = sb("wv_cur", P, KC, HG * HD)
        bv_cur = sb("bv_cur", HG * HD, 1)
        xnT_all = sb("xnT_all", P, 2 * KC * T)
        xnT = sb("xnT", P, KC, T)
        QT = sb("QT", P, T)
        KT = sb("KT", P, T)
        VT = sb("VT", HG * HD, T)
        V1 = sb("V1", P, TPB, HG, 2 * HD)
        cT = sb("cT", P, P)
        S = sb("S", P, RING, T)
        W = sb("W", P, 2, 2, T)
        M8 = sb("M8", P, RING, 8 * ROUNDS)
        NM = sb("NM", P, RING, 1)
        MK = sb("MK", P, T)
        EX = sb("EX", P, 2, T)
        PR = sb("PR", P, 2, T)
        PTs = sb("PTs", P, 2, T)
        ctxr = sb("ctxr", P, 2, GROUPS, TPB * CTXW)
        x1r = sb("x1r", P, RINGX, D)
        crec = sb("crec", P, GROUPS, HG)
        ctxn = sb("ctxn", P, GROUPS, HG, HD)
        ctxT = sb("ctxT", P, KC, P)

        class Job:
            def __init__(self, n):
                self.n = n
                self.x = sb(f"x_{n}", P, D)
                self.st = sb(f"st_{n}", P, 6)
                self.mv = sb(f"mv_{n}", P, 2)
                self.ve = sb(f"ve_{n}", P, 1)
                self.rstd = sb(f"rstd_{n}", P, 1)
                self.h = sb(f"h_{n}", P, D)
                self.junk = sb(f"junk_{n}", P, D)
                self.ss = sb(f"ss_{n}", P, 1)
                self.nmr = sb(f"nmr_{n}", P, 1)
                self.rinv = sb(f"rinv_{n}", P, 1)
                self.hT = sb(f"hT_{n}", P, KC, P)
                self.L = sb(f"L_{n}", P, E)
                self.v8 = sb(f"v8_{n}", P, 8)
                self.mr8 = sb(f"mr8_{n}", P, 8)
                self.R = sb(f"R_{n}", P, E)
                self.fb = sb(f"fb_{n}", P, E)
                self.na = sb(f"na_{n}", P, 1)
                self.pos = sb(f"pos_{n}", P, E)
                self.fb2 = sb(f"fb2_{n}", P, E)
                self.mk = sb(f"mk_{n}", P, E)
                self.RL = sb(f"RL_{n}", P, E)
                self.nv = sb(f"nv_{n}", P, 1)
                self.eg = sb(f"eg_{n}", P, E)
                self.em = sb(f"em_{n}", P, E)
                self.gs = sb(f"gs_{n}", P, 1)
                self.rgs = sb(f"rgs_{n}", P, 1)
                self.rw = sb(f"rw_{n}", P, E)
                self.MX = sb(f"MX_{n}", P, E, QKV)
                self.qk = sb(f"qk_{n}", P, 2 * ED)
                self.vall = sb(f"vall_{n}", P, TPB, ED)
                self.qT = sb(f"qT_{n}", P, P)
                self.kT = sb(f"kT_{n}", P, T)
                self.maskc = sb(f"maskc_{n}", P, T)
                self.Sf = sb(f"Sf_{n}", P, T)
                self.mxr = sb(f"mxr_{n}", P, 1)
                self.nm = sb(f"nm_{n}", P, 1)
                self.Pf = sb(f"Pf_{n}", P, T)
                self.rs = sb(f"rs_{n}", P, 1)
                self.rrs = sb(f"rrs_{n}", P, 1)
                self.PTf = sb(f"PTf_{n}", P, T)
                self.rwn = sb(f"rwn_{n}", P, E)
                self.att = sb(f"att_{n}", P, ED)
                self.mix = sb(f"mix_{n}", P, E, ED)
                self.mixT = sb(f"mixT_{n}", P, E * ED // P, P)
                self.y = sb(f"y_{n}", P, D)

        jobs = {n: Job(n) for n in "ab"}
        for n, J in jobs.items():
            J.F = None
            J.sem = {k: sem(f"{k}_{n}") for k in (
                "x_in", "x_bn", "x_var", "x_rstd", "x_bias", "x_eps", "h_guard", "gate_rec", "sc_rec", "h_norm", "h_sq", "hT_ps", "hT_sb", "lg_ps", "h_rinv",
                "lg", "lg_top", "lg_pair", "lg_repl", "gate", "gate_exp", "gate_em", "gate_sum", "rw",
                "qkv_ps", "qkv_sc", "qkv_add", "qk_ready", "v_ready", "qkT_ps", "qkT_sb", "mask_c",
                "sc_ps", "sc_max", "sc_nmax", "sc_exp", "pT_ps", "pT_sb", "pv_ps", "att_sb", "rw_sum",
                "mix", "mixT_ps", "mixT_sb", "y_ps", "y_out")}
        jobs["a"].sem.update({k: sem(k) for k in ("ctx_rec", "ctx_norm", "ctxT_ps", "ctxT_sb", "op_ps", "out_st")})
        jobs["b"].sem.update({k: sem(k) for k in ("y_bn", "y_var", "y_rstd", "y_bias", "y_eps", "y_ring", "xn_norm", "xn_ps", "xn_sb")})
        stx = sb("stx", P, 6)
        mvx = sb("mvx", P, 2)
        rstdx = sb("rstdx", P, 1)
        nmrx = sb("nmrx", P, 1)
        vex = sb("vex", P, 1)
        xn = sb("xn", P, D)

        pS = [bank("pS0"), bank("pS1")]
        pT = [bank("pT0"), bank("pT1")]
        pO = bank("pO")
        pG = bank("pG")
        jobs["a"].F = bank("pFa")
        jobs["b"].F = bank("pFb")

        s_ld = sem("s_ld")
        s_cst = sem("s_cst")
        s_const = sem("s_const")
        s_passed = {e.engine: sem(f"s_passed_{n}") for n, e in (("pe", nc.tensor), ("dve", nc.vector),
                                                                ("pool", nc.gpsimd))}
        s_ini = sem("s_ini")
        s_simsq, s_simps, s_simg, s_simr, s_simn = (sem("s_simsq"), sem("s_simps"), sem("s_simg"), sem("s_simr"),
                                                    sem("s_simn"))
        s_gexp, s_gadd, s_grec, s_gps, s_sig = (sem("s_gexp"), sem("s_gadd"), sem("s_grec"), sem("s_gps"),
                                                sem("s_sig"))
        s_w = sem("s_w")
        s_xc = sem("s_xc")
        s_qp, s_qe = sem("s_qp"), sem("s_qe")
        s_kp, s_ke = sem("s_kp"), sem("s_ke")
        s_vt, s_vte = sem("s_vt"), sem("s_vte")
        s_vp, s_ve = sem("s_vp"), sem("s_ve")
        s_sc = sem("s_sc")
        s_ev = sem("s_ev")
        s_tk = sem("s_tk")
        s_nm = sem("s_nm")
        s_ex = sem("s_ex")
        s_ge = sem("s_ge")
        s_pr = sem("s_pr")
        s_pt = sem("s_pt")
        s_pe = sem("s_pe")
        s_pv = sem("s_pv")
        s_oc = sem("s_oc")
        s_ot = sem("s_ot")
        s_o = sem("s_o")
        PASSES = 2 * ROUNDS - 1

        block = ctx.enter_context(nc.Block())

        def wait(eng, s, v):
            if not isinstance(v, int) or v > 0:
                eng.wait_ge(s, v)

        def held(eng, *counts):
            for s, v in counts:
                wait(eng, s, v)
            eng.sem_inc(s_passed[eng.engine], 1)

        def emit(eng, step, tail=None):
            step(eng, None, False, False, None, 0, None)
            with eng.Fori(1, LAG_B - 1) as t:
                step(eng, None, False, False, None, t, None)
            step(eng, None, False, False, None, LAG_B - 1, 0)
            step(eng, 0, True, False, None, LAG_B, 1)
            with eng.Fori(1, LAG_A) as s:
                step(eng, s, True, True, None, s + LAG_B, s + 1)
            step(eng, LAG_A, True, True, 0, LAG_A + LAG_B, LAG_A + 1)
            with eng.Fori(LAG_A + 1, STEPS - LAG_B) as s:
                step(eng, s, True, True, s - LAG_A, s + LAG_B, s + 1)
            with eng.Fori(STEPS - LAG_B, STEPS) as s:
                step(eng, s, True, True, s - LAG_A, None, s + 1)
            step(eng, STEPS, False, True, STEPS - LAG_A, None, None)
            with eng.Fori(STEPS + 1 - LAG_A, TILES) as t:
                step(eng, None, False, False, t, None, None)

        def both(ta, tb, j):
            return [(jobs[n], t, j - START[n]) for n, t in (("a", ta), ("b", tb)) if t is not None]

        def lagged(s, j, lag, attn, prev):
            if (j >= lag and not attn) or (j < lag and not prev):
                return None
            return s * UNITS + (j - lag)

        x_t = x.rearrange("b (n p) d -> (b n) p d", p=P)
        out_t = out.rearrange("b (n p) d -> (b n) p d", p=P)
        LOADS = 6

        @block.sync
        def _(sp):
            sp.dma_start(simn[:], sim.rearrange("(c p) e -> p c e", p=P)).then_inc(s_ld, 16)
            sp.dma_start(gate_row[:, 0, :], gates).then_inc(s_ld, 16)
            sp.dma_start(jobs["b"].x[:], x_t[0]).then_inc(jobs["b"].sem["x_in"], 16)
            sp.dma_start(wf_sb[:], wf).then_inc(s_ld, 16)
            sp.dma_start(wof_sb[:], wof).then_inc(s_ld, 16)
            sp.dma_start(wo_sb[:], wo).then_inc(s_ld, 16)
            sp.dma_start(bo_row[:], bo).then_inc(s_ld, 16)

            def step(sp, s, attn, prev, ta, tb, nx):
                if nx is not None:
                    wait(sp, s_ke, nx)
                    wait(sp, s_vte, nx)
                    sp.dma_start(wqk_cur[:], wqk[ds(nx % GROUPS, 1)].rearrange("a p c m -> p (a c) m")
                                 ).then_inc(s_w, 16)
                    sp.dma_start(wv_cur[:], wv[ds(nx % GROUPS, 1)].rearrange("a p c m -> p (a c) m")
                                 ).then_inc(s_w, 16)
                    sp.dma_start(bv_cur[:], bv[ds(nx % GROUPS, 1)].rearrange("a p c -> p (a c)")
                                 ).then_inc(s_w, 16)
                    sp.dma_start(bqk_cur[:], bqk[ds(nx % GROUPS, 1)].rearrange("a p c -> p (a c)")
                                 ).then_inc(s_w, 16)
                    wait(sp, s_vt, nx)
                    if nx is not None and not (isinstance(nx, int) and nx >= STEPS):
                        nb = nx // GROUPS
                    wait(sp, jobs["b"].sem["xn_sb"], nb * TPB + TPB if tb is not None else TILES)
                    sp.dma_start(xnT[:], xnT_all[:, ds((nb % 2) * KC * T, KC * T)]
                                 .rearrange("p (c t) -> p c t", c=KC)).then_inc(s_xc, 16)
                if tb is not None:
                    J = jobs["b"]
                    if isinstance(tb, int) or True:
                        sp.wait_ge(J.sem["y_out"], tb + 1)
                        nxt = min(tb + 1, TILES - 1) if isinstance(tb, int) else (tb + 1) % TILES
                        sp.dma_start(J.x[:], x_t[ds(nxt, 1)].rearrange("a p d -> (a p) d")
                                     ).then_inc(J.sem["x_in"], 16)
                if ta is not None:
                    J = jobs["a"]
                    sp.wait_ge(J.sem["y_out"], ta + 1)
                    sp.dma_start(out_t[ds(ta, 1)].rearrange("a p d -> (a p) d"), J.y[:]
                                 ).then_inc(J.sem["out_st"], 16)

            emit(sp, step)
            sp.wait_ge(jobs["a"].sem["out_st"], 16 * TILES)
            sp.wait_ge(jobs["b"].sem["x_in"], 16 * (TILES + 1))

        @block.tensor
        def _(pe):
            pe.wait_ge(s_ld, 16 * LOADS)
            pe.wait_ge(s_cst, 3)
            pe.wait_ge(s_simsq, 1)
            for c in range(KC):
                mm = nc.tensor.matmul(pG[:, 0:E], ones[:], simsq[:, c, :], start=c == 0, stop=c == KC - 1)
            mm.then_inc(s_simps, 1)
            pe.wait_ge(s_grec, 1)
            nc.tensor.matmul(pO[:, 0:E], ones[0:1, :], gate_row[:, 3, :], start=True, stop=True).then_inc(s_gps, 1)
            pe.wait_ge(s_simr, 1)
            pe.wait_ge(s_sig, 1)
            pe.wait_ge(s_simn, 1)
            pe.wait_ge(s_ini, 4)

            def ffn(J, t, r, part):
                q = J.sem
                F = J.F
                if J.n == "a" and (r, part) == (-1, 2):
                    pe.wait_ge(q["ctx_norm"], t + 1)
                    wait(pe, q["y_out"], t)
                    cn = ctxn[:].rearrange("p g h d -> p (g h d)")
                    for c in range(KC):
                        mm = nc.tensor.transpose(F[:, c * P:(c + 1) * P], cn[:, c * P:(c + 1) * P], ident[:])
                    mm.then_inc(q["ctxT_ps"], 1)
                if J.n == "a" and (r, part) == (0, 1):
                    pe.wait_ge(q["ctxT_sb"], t + 1)
                    for c in range(KC):
                        nc.tensor.matmul(F[:, 0:D], ctxT[:, c, :], wo_sb[:, c, :], start=c == 0, stop=False)
                    nc.tensor.matmul(F[:, 0:D], ones[0:1, :], bo_row[:], start=False, stop=True
                                     ).then_inc(q["op_ps"], 1)
                if (r, part) == (1, 2):
                    pe.wait_ge(q["h_norm"], t + 1)
                    if J.n == "b":
                        wait(pe, q["xn_sb"], t)
                    else:
                        pe.wait_ge(q["x_in"], t + 1)
                    for c in range(KC):
                        mm = nc.tensor.transpose(F[:, c * P:(c + 1) * P], J.h[:, c * P:(c + 1) * P], ident[:])
                    mm.then_inc(q["hT_ps"], 1)
                if (r, part) == (2, 1):
                    pe.wait_ge(q["hT_sb"], t + 1)
                    for c in range(KC):
                        mm = nc.tensor.matmul(F[:, 0:E], J.hT[:, c, :], simn[:, c, :], start=c == 0,
                                              stop=c == KC - 1)
                    mm.then_inc(q["lg_ps"], 1)
                if 3 <= r <= 6:
                    c2 = 2 * (r - 3) + part - 1
                    if c2 == 0:
                        pe.wait_ge(q["lg"], t + 1)
                    else:
                        pe.wait_ge(q["qkv_sc"], t * CHUNKS + c2)
                    for c in range(KC):
                        mm = nc.tensor.matmul(F[:, 0:2 * QKV], J.hT[:, c, :],
                                              wf_sb[:, c, c2 * 2 * QKV:(c2 + 1) * 2 * QKV],
                                              start=c == 0, stop=c == KC - 1)
                    mm.then_inc(q["qkv_ps"], 1)
                if (r, part) == (8, 1):
                    held(pe, (q["qk_ready"], t + 1))
                    for c in range(2):
                        mm = nc.tensor.transpose(F[0:ED, c * P:(c + 1) * P], J.qk[:, c * ED:(c + 1) * ED], ident[:])
                    mm.then_inc(q["qkT_ps"], 1)
                if (r, part) == (8, 2):
                    pe.wait_ge(q["qkT_sb"], t + 1)
                    nc.tensor.matmul(F[:, :], J.qT[0:ED, :], J.kT[0:ED, :], start=True, stop=True
                                     ).then_inc(q["sc_ps"], 1)
                if (r, part) == (10, 2):
                    pe.wait_ge(q["sc_exp"], t + 1)
                    for c in range(TPB):
                        mm = nc.tensor.transpose(F[:, c * P:(c + 1) * P], J.Pf[:, c * P:(c + 1) * P], ident[:])
                    mm.then_inc(q["pT_ps"], 1)
                if (r, part) == (11, 1):
                    pe.wait_ge(q["pT_sb"], t + 1)
                    pe.wait_ge(q["v_ready"], t + 1)
                    for c in range(TPB):
                        mm = nc.tensor.matmul(F[:, 0:ED], J.PTf[:, c * P:(c + 1) * P], J.vall[:, c, :],
                                              start=c == 0, stop=c == TPB - 1)
                    mm.then_inc(q["pv_ps"], 1)
                if r == 12:
                    if part == 1:
                        pe.wait_ge(q["mix"], t + 1)
                    else:
                        pe.wait_ge(q["mixT_sb"], 2 * t + 1)
                    mx = J.mix[:].rearrange("p e d -> p (e d)")
                    for c in range(4):
                        k = 4 * (part - 1) + c
                        mm = nc.tensor.transpose(F[:, c * P:(c + 1) * P], mx[:, k * P:(k + 1) * P], ident[:])
                    mm.then_inc(q["mixT_ps"], 1)
                if (r, part) == (13, 1):
                    pe.wait_ge(q["mixT_sb"], 2 * t + 2)
                    for c in range(E * ED // P):
                        mm = nc.tensor.matmul(F[:, 0:D], J.mixT[:, c, :], wof_sb[:, c, :], start=c == 0,
                                              stop=c == E * ED // P - 1)
                    mm.then_inc(q["y_ps"], 1)
                if J.n == "b" and (r, part) == (14, 2):
                    pe.wait_ge(q["xn_norm"], t + 1)
                    for c in range(KC):
                        mm = nc.tensor.transpose(F[:, c * P:(c + 1) * P], xn[:, c * P:(c + 1) * P], ident[:])
                    mm.then_inc(q["xn_ps"], 1)

            def step(pe, s, attn, prev, ta, tb, nx):
                for j in range(SLOTS):
                    qt, hh = divmod(j, HG)
                    if attn:
                        u = s * UNITS + j
                        if j == 0:
                            pe.wait_ge(s_ke, s + 1)
                        wait(pe, s_ev, u - 1)
                        r0 = 32 * hh
                        nc.tensor.matmul(pS[j % 2][:], QT[r0:r0 + HD, qt * P:(qt + 1) * P], KT[r0:r0 + HD, :],
                                         start=True, stop=True).then_inc(s_sc, 1)
                    for J, t, r in both(ta, tb, j):
                        ffn(J, t, r, 1)
                    u = lagged(s, j, OUT_LAG, attn, prev)
                    if u is not None:
                        lj = (j - OUT_LAG) % SLOTS
                        pe.wait_ge(s_pr, u + 1)
                        wait(pe, s_pe, u - 1)
                        for c in range(TPB):
                            mm = nc.tensor.transpose(pT[lj % 2][:, c * P:(c + 1) * P],
                                                     PR[:, lj % 2, c * P:(c + 1) * P], ident[:])
                        mm.then_inc(s_pt, 1)
                    if lagged(s, j, CTX_LAG, attn, prev) is not None and (j - CTX_LAG) % HG == HG - 1:
                        lq = (j - CTX_LAG) % SLOTS // HG
                        n = (s if j >= CTX_LAG else s - 1) * TPB + lq
                        pe.wait_ge(s_oc, n + 1)
                        wait(pe, s_o, n)
                        if lq == 2:
                            pe.wait_ge(s_ke, s + 1)
                        elif attn:
                            pe.wait_ge(s_ve, s + 1)
                        nc.tensor.transpose(pG[:, 0:P], cT[:], ident[:]).then_inc(s_ot, 1)
                    for J, t, r in both(ta, tb, j):
                        ffn(J, t, r, 2)
                    if attn and j == 4:
                        held(pe, (s_vte, s + 1))
                        w = HG * HD
                        for n in range(TPB):
                            mm = nc.tensor.transpose(pG[:, n * w:(n + 1) * w], VT[:, n * P:(n + 1) * P],
                                                     ident[0:w, 0:w])
                        mm.then_inc(s_vp, 1)
                    if u is not None:
                        lq, lh = divmod(lj, HG)
                        if lj == 0:
                            pe.wait_ge(s_ve, s + 1)
                        if lh == 0:
                            wait(pe, s_oc, (s if j >= OUT_LAG else s - 1) * TPB + lq)
                        pe.wait_ge(s_pe, u + 1)
                        for c in range(TPB):
                            mm = nc.tensor.matmul(pO[32 * lh:32 * lh + 32, 0:P], V1[:, c, lh, :],
                                                  PTs[:, lj % 2, c * P:(c + 1) * P],
                                                  start=c == 0, stop=c == TPB - 1)
                        mm.then_inc(s_pv, 1)
                    if attn and j == 3:
                        pe.wait_ge(s_ke, s + 1)
                        wait(pe, s_o, s * TPB - 1)
                        for c in range(KC):
                            mm = nc.tensor.matmul(pG[0:HG * HD, :], wv_cur[:, c, :], xnT[:, c, :],
                                                  start=c == 0, stop=c == KC - 1)
                        mm.then_inc(s_vt, 1)
                    if nx is not None and j == 14:
                        pe.wait_ge(s_w, 64 * (nx + 1))
                        pe.wait_ge(s_xc, 16 * (nx + 1))
                        if attn:
                            pe.wait_ge(s_o, s * TPB + 2)
                        for c in range(KC):
                            mm = nc.tensor.matmul(pG[:, :], wqk_cur[:, c, :], xnT[:, c, :], start=c == 0,
                                                  stop=c == KC - 1)
                        mm.then_inc(s_qp, 1)
                    if nx is not None and j == 15:
                        pe.wait_ge(s_qe, nx + 1)
                        for c in range(KC):
                            mm = nc.tensor.matmul(pG[:, :], wqk_cur[:, KC + c, :], xnT[:, c, :], start=c == 0,
                                                  stop=c == KC - 1)
                        mm.then_inc(s_kp, 1)

            emit(pe, step)

        @block.scalar
        def _(act):
            act.wait_ge(s_ld, 16 * LOADS)
            nc.scalar.activation(gate_row[:, 1, :], gate_row[:, 0, :], ACT.Exp, scale=-1.0).then_inc(s_gexp, 1)
            act.wait_ge(s_gps, 1)
            nc.scalar.copy(sig[:], pO[:, 0:E]).then_inc(s_sig, 1)

            def ffn(J, t, r, part):
                q = J.sem
                F = J.F
                if J.n == "a" and (r, part) == (-1, 2):
                    act.wait_ge(q["ctxT_ps"], t + 1)
                    nc.scalar.copy(ctxT[:], F[:, 0:D].rearrange("p (c t) -> p c t", c=KC)).then_inc(q["ctxT_sb"], 1)
                if (r, part) == (1, 1):
                    act.wait_ge(q["x_bias"], t + 1)
                    nc.scalar.activation(J.h[:], J.x[:], ACT.Identity, scale=J.rstd[:], bias=J.nmr[:]
                                         ).then_inc(q["h_norm"], 1)
                    act.wait_ge(q["h_norm"], t + 1)
                    nc.scalar.activation(J.junk[:], J.h[:], ACT.Square, accum_out=J.ss[:]).then_inc(q["h_sq"], 1)
                if (r, part) == (1, 2):
                    act.wait_ge(q["hT_ps"], t + 1)
                    nc.scalar.copy(J.hT[:], F[:, 0:D].rearrange("p (c t) -> p c t", c=KC)).then_inc(q["hT_sb"], 1)
                if (r, part) == (3, 1):
                    act.wait_ge(q["gate"], 7 * t + 7)
                    nc.scalar.activation(J.eg[:], J.RL[:], ACT.Exp, bias=J.nv[:]).then_inc(q["gate_exp"], 1)
                    act.wait_ge(q["gate_em"], t + 1)
                    nc.scalar.activation(J.junk[:, 0:E], J.em[:], ACT.Copy, accum_out=J.gs[:]
                                         ).then_inc(q["gate_sum"], 1)
                    act.wait_ge(q["rw"], t + 1)
                if 3 <= r <= 6:
                    c2 = 2 * (r - 3) + part - 1
                    act.wait_ge(q["qkv_ps"], t * CHUNKS + c2 + 1)
                    for k in range(2):
                        e = 2 * c2 + k
                        ins = nc.scalar.activation(J.MX[:, e, :], F[:, k * QKV:(k + 1) * QKV], ACT.Copy,
                                                   scale=J.rw[:, e:e + 1])
                    ins.then_inc(q["qkv_sc"], 1)
                if (r, part) == (8, 1):
                    act.wait_ge(q["qkT_ps"], t + 1)
                    nc.scalar.copy(J.qT[0:ED, :], F[0:ED, 0:P])
                    nc.scalar.copy(J.kT[0:ED, ds((t % TPB) * P, P)], F[0:ED, P:2 * P]).then_inc(q["qkT_sb"], 1)
                if (r, part) == (8, 2):
                    nc.scalar.copy(J.maskc[:], maskw[:, ds((TPB - 1 - t % TPB) * P, T)]).then_inc(q["mask_c"], 1)
                if (r, part) == (10, 1):
                    act.wait_ge(q["sc_nmax"], t + 1)
                    nc.scalar.activation(J.Pf[:], J.Sf[:], ACT.Exp, bias=J.nm[:], scale=ED ** -0.5,
                                         accum_out=J.rs[:]).then_inc(q["sc_exp"], 1)
                if (r, part) == (10, 2):
                    act.wait_ge(q["pT_ps"], t + 1)
                    nc.scalar.copy(J.PTf[:], F[:]).then_inc(q["pT_sb"], 1)
                if (r, part) == (11, 1):
                    act.wait_ge(q["pv_ps"], t + 1)
                    nc.scalar.copy(J.att[:], F[:, 0:ED]).then_inc(q["att_sb"], 1)
                if r == 12:
                    act.wait_ge(q["mixT_ps"], 2 * t + part)
                    nc.scalar.copy(J.mixT[:, 4 * (part - 1):4 * part, :], F[:].rearrange("p (c t) -> p c t", c=4)
                                   ).then_inc(q["mixT_sb"], 1)
                if J.n == "b" and (r, part) == (14, 1):
                    act.wait_ge(q["y_bias"], t + 1)
                    nc.scalar.activation(xn[:], J.y[:], ACT.Identity, scale=rstdx[:], bias=nmrx[:]
                                         ).then_inc(q["xn_norm"], 1)
                    nc.scalar.copy(x1r[:, ds(t % RINGX, 1), :].rearrange("p a d -> p (a d)"), J.y[:]
                                   ).then_inc(q["y_ring"], 1)
                if J.n == "b" and (r, part) == (14, 2):
                    act.wait_ge(q["xn_ps"], t + 1)
                    if isinstance(t, int):
                        wait(act, s_xc, 16 * (t - LAG_B + 1))
                    elif t.min_val >= LAG_B:
                        act.wait_ge(s_xc, (t - LAG_B + 1) * 16)
                    off = ((t // TPB) % 2) * (KC * T) + (t % TPB) * P
                    for c in range(KC):
                        ins = nc.scalar.copy(xnT_all[:, ds(off + c * T, P)], F[:, c * P:(c + 1) * P])
                    ins.then_inc(q["xn_sb"], 1)

            def step(act, s, attn, prev, ta, tb, nx):
                for j in range(SLOTS):
                    if attn:
                        u = s * UNITS + j
                        act.wait_ge(s_sc, u + 1)
                        wait(act, s_pr, u + 1 - RING)
                        nc.scalar.copy(S[:, j % RING, :], pS[j % 2][:]).then_inc(s_ev, 1)
                    u = lagged(s, j, EXP_LAG, attn, prev)
                    if u is not None:
                        lj = (j - EXP_LAG) % SLOTS
                        act.wait_ge(s_nm, u + 1)
                        wait(act, s_pr, u - 1)
                        nc.scalar.activation(EX[:, lj % 2, :], S[:, lj % RING, :], ACT.Exp, bias=NM[:, lj % RING, :],
                                             scale=HD ** -0.5).then_inc(s_ex, 1)
                    for J, t, r in both(ta, tb, j):
                        ffn(J, t, r, 1)
                    u = lagged(s, j, OUT_LAG, attn, prev)
                    if u is not None:
                        lj = (j - OUT_LAG) % SLOTS
                        act.wait_ge(s_pt, u + 1)
                        wait(act, s_pv, u - 1)
                        nc.scalar.copy(PTs[:, lj % 2, :], pT[lj % 2][:]).then_inc(s_pe, 1)
                    if lagged(s, j, CTX_LAG, attn, prev) is not None and (j - CTX_LAG) % HG == HG - 1:
                        lq = (j - CTX_LAG) % SLOTS // HG
                        ls = s if j >= CTX_LAG else s - 1
                        if not isinstance(ls, int) and ls.min_val > LAG_A:
                            act.wait_ge(jobs["a"].sem["ctx_norm"], ls - LAG_A)
                        act.wait_ge(s_ot, ls * TPB + lq + 1)
                        nc.scalar.copy(ctxr[:, ds((ls // GROUPS) % 2, 1), ds(ls % GROUPS, 1),
                                            lq * CTXW:(lq + 1) * CTXW].rearrange("p a g (h e) -> p (a g h) e", h=HG),
                                       pG[:, 0:P].rearrange("p (h e) -> p h e", h=HG)[:, :, 0:HD + 1]
                                       ).then_inc(s_o, 1)
                    for J, t, r in both(ta, tb, j):
                        ffn(J, t, r, 2)
                    if u is not None and lj % HG == HG - 1:
                        n = (s if j >= OUT_LAG else s - 1) * TPB + lj // HG
                        act.wait_ge(s_pv, u + 1)
                        wait(act, s_ot, n)
                        nc.scalar.copy(cT[:], pO[:, 0:P]).then_inc(s_oc, 1)
                    if attn and j == 3:
                        act.wait_ge(s_vt, s + 1)
                        nc.scalar.activation(VT[:], pG[0:HG * HD, :], ACT.Identity, bias=bv_cur[:]).then_inc(s_vte, 1)
                    if attn and j == 4:
                        act.wait_ge(s_vp, s + 1)
                        wait(act, s_pv, s * UNITS)
                        nc.scalar.copy(V1[:, :, :, 0:HD],
                                       pG[:, 0:D].rearrange("p (n h d) -> p n h d", n=TPB, h=HG)).then_inc(s_ve, 1)
                    if nx is not None and j == 15:
                        act.wait_ge(s_qp, nx + 1)
                        if attn:
                            act.wait_ge(s_sc, (s + 1) * UNITS)
                        nc.scalar.activation(QT[:], pG[:], ACT.Identity, bias=bqk_cur[:, 0:1]).then_inc(s_qe, 1)
                        act.wait_ge(s_kp, nx + 1)
                        nc.scalar.activation(KT[:], pG[:], ACT.Identity, bias=bqk_cur[:, 1:2]).then_inc(s_ke, 1)

            emit(act, step)

        @block.vector
        def _(dve):
            nc.vector.memset(V1[:], 0.0).then_inc(s_ini, 1)
            dve.wait_ge(s_ini, 1)
            nc.vector.memset(V1[:, :, :, HD:HD + 1], 1.0)
            for n in "ab":
                J = jobs[n]
                nc.vector.memset(J.mr8[:], BIG)
                nc.vector.memset(J.kT[:], 0.0)
                ins = nc.vector.memset(J.vall[:], 0.0)
                ins.then_inc(s_ini, 1)
            dve.wait_ge(s_ld, 16 * LOADS)
            nc.vector.tensor_tensor(simsq[:], simn[:], simn[:], ALU.mult).then_inc(s_simsq, 1)
            dve.wait_ge(s_gexp, 1)
            nc.vector.tensor_scalar(gate_row[:, 2, :], gate_row[:, 1, :], 1.0, None, ALU.add).then_inc(s_gadd, 1)
            dve.wait_ge(s_gadd, 1)
            nc.vector.reciprocal(gate_row[:, 3, :], gate_row[:, 2, :]).then_inc(s_grec, 1)
            dve.wait_ge(s_simps, 1)
            nc.vector.tensor_scalar(simg[:], pG[:, 0:E], 1e-24, None, ALU.max).then_inc(s_simg, 1)
            dve.wait_ge(s_simr, 1)
            for c in range(KC):
                ins = nc.vector.tensor_tensor(simn[:, c, :], simn[:, c, :], simr[:], ALU.mult)
            ins.then_inc(s_simn, 1)
            dve.wait_ge(s_ini, 3)
            nc.vector.memset(M8[:], 0.0).then_inc(s_ini, 1)
            dve.wait_ge(s_ini, 4)
            dve.wait_ge(s_cst, 3)
            nc.vector.memset(M8[:], 0.0).then_inc(s_const, 1)
            dve.wait_ge(s_sig, 1)

            def stats(src, st, mv, q, k, t):
                nc.vector.bn_stats(st[:], src[:]).then_inc(q[k + "_bn"], 1)
                held(dve, (q[k + "_bn"], t + 1))
                nc.vector.bn_aggr(mv[:], st[:]).then_inc(q[k + "_var"], 1)

            def ffn(J, t, r):
                q = J.sem
                F = J.F
                if J.n == "a" and r == -2:
                    dve.wait_ge(s_o, (t // TPB) * (GROUPS * TPB) + GROUPS * TPB)
                    c = ctxr[:, ds((t // TPB) % 2, 1), :, ds((t % TPB) * CTXW, CTXW)].rearrange(
                        "p a g (h e) -> p (a g) h e", h=HG)
                    nc.vector.reciprocal(crec[:], c[:, :, :, HD]).then_inc(q["ctx_rec"], 1)
                if r == 0:
                    if J.n == "a":
                        dve.wait_ge(q["op_ps"], t + 1)
                        nc.vector.tensor_tensor(J.x[:], F[:, 0:D],
                                                x1r[:, ds(t % RINGX, 1), :].rearrange("p a d -> p (a d)"),
                                                ALU.add).then_inc(q["x_in"], 1)
                        dve.wait_ge(q["x_in"], t + 1)
                    else:
                        dve.wait_ge(q["x_in"], (t + 1) * 16)
                    stats(J.x, J.st, J.mv, q, "x", t)
                if r == 2:
                    dve.wait_ge(q["h_rinv"], t + 1)
                    dve.wait_ge(q["lg_ps"], t + 1)
                    nc.vector.scalar_tensor_tensor(out=J.L[:], in0=F[:, 0:E], scalar=J.rinv[:], in1=sig[:],
                                                   op0=ALU.mult, op1=ALU.subtract).then_inc(q["lg"], 1)
                    held(dve, (q["lg"], t + 1))
                    nc.vector.max(J.v8[:], J.L[:]).then_inc(q["lg_top"], 1)
                    dve.wait_ge(q["lg_top"], t + 1)
                    nc.vector.tensor_copy(J.mr8[:, 0:2], J.v8[:, 0:2]).then_inc(q["lg_pair"], 1)
                    held(dve, (q["lg_pair"], t + 1))
                    nc.vector.match_replace(J.R[:], J.mr8[:], J.L[:], -BIG).then_inc(q["lg_repl"], 1)
                if r == 9:
                    held(dve, (q["mask_c"], t + 1), (q["sc_ps"], t + 1))
                    nc.vector.tensor_tensor_reduce(out=J.Sf[:], in0=F[:], in1=J.maskc[:], scale=1.0, scalar=-BIG,
                                                   op0=ALU.add, op1=ALU.max, accum_out=J.mxr[:]
                                                   ).then_inc(q["sc_max"], 1)
                if r == 13:
                    dve.wait_ge(q["y_ps"], t + 1)
                    if J.n == "a":
                        wait(dve, q["out_st"], t * 16)
                    else:
                        wait(dve, q["y_ring"], t)
                        wait(dve, q["xn_norm"], t)
                    nc.vector.scalar_tensor_tensor(out=J.y[:], in0=F[:, 0:D], scalar=0.5, in1=J.x[:],
                                                   op0=ALU.mult, op1=ALU.add).then_inc(q["y_out"], 1)
                    if J.n == "b":
                        dve.wait_ge(q["y_out"], t + 1)
                        stats(J.y, stx, mvx, q, "y", t)

            def step(dve, s, attn, prev, ta, tb, nx):
                for j in range(SLOTS):
                    u = lagged(s, j, TOP_LAG, attn, prev)
                    if u is not None and j % 2 == 1:
                        done = u * PASSES
                        src = [S[:, (j - TOP_LAG + i) % RING, :] for i in range(2)]
                        for k in range(PASSES):
                            for i in range(2):
                                m = M8[:, (j - TOP_LAG + i) % RING, k // 2 * 8:k // 2 * 8 + 8]
                                if k == 0:
                                    held(dve, (s_ev, u + i + 1))
                                else:
                                    held(dve, (s_tk, done + 2 * k + i - 1))
                                if k % 2 == 0:
                                    nc.vector.max(m, src[i]).then_inc(s_tk, 1)
                                else:
                                    to = W[:, i, k // 2 % 2, :]
                                    nc.vector.match_replace(to, m, src[i], -BIG).then_inc(s_tk, 1)
                                    src[i] = to
                    for J, t, r in both(ta, tb, j):
                        ffn(J, t, r)

            emit(dve, step)

        @block.gpsimd
        def _(pool):
            nc.gpsimd.memset(ident[:], 0.0).then_inc(s_cst, 1)
            nc.gpsimd.memset(ones[:], 1.0)
            nc.gpsimd.memset(minus_half[:], -0.5)
            nc.gpsimd.memset(minus_one[:], -1.0)
            nc.gpsimd.memset(maskw[:], 0.0).then_inc(s_cst, 1)
            pool.wait_ge(s_cst, 2)
            nc.gpsimd.affine_select(out=maskw[:], in_=maskw[:], compare_op=ALU.is_ge, fill=MASKED,
                                    base=(TPB - 1) * P, pattern=[[-1, (2 * TPB - 1) * P]], channel_multiplier=1)
            nc.gpsimd.affine_select(out=ident[:], in_=ident[:], compare_op=ALU.not_equal, fill=1.0, base=0,
                                    pattern=[[-1, P]], channel_multiplier=1).then_inc(s_cst, 1)
            pool.wait_ge(s_cst, 3)
            pool.wait_ge(s_simg, 1)
            nc.gpsimd.tensor_tensor(simr[:], simg[:], minus_half[:], ALU.pow).then_inc(s_simr, 1)

            def rsqrt(guarded, src, floor, op, out, src_ready, guard_ready, out_ready, t):
                held(pool, (src_ready, t + 1))
                nc.gpsimd.tensor_scalar(guarded[:], src, floor, None, op).then_inc(guard_ready, 1)
                pool.wait_ge(guard_ready, t + 1)
                nc.gpsimd.tensor_tensor(out[:], guarded[:], minus_half[:, 0:1], ALU.pow).then_inc(out_ready, 1)

            def ffn(J, t, r):
                q = J.sem
                if J.n == "a" and r == -1:
                    pool.wait_ge(q["ctx_rec"], t + 1)
                    c = ctxr[:, ds((t // TPB) % 2, 1), :, ds((t % TPB) * CTXW, CTXW)].rearrange(
                        "p a g (h e) -> p (a g) h e", h=HG)
                    nc.gpsimd.tensor_tensor(ctxn[:], c[:, :, :, 0:HD],
                                            crec[:].unsqueeze(3).broadcast_to([P, GROUPS, HG, HD]),
                                            ALU.mult).then_inc(q["ctx_norm"], 1)
                if r == 1:
                    rsqrt(J.ve, J.mv[:, 1:2], 1e-5, ALU.add, J.rstd, q["x_var"], q["x_eps"], q["x_rstd"], t)
                    held(pool, (q["x_rstd"], t + 1))
                    nc.gpsimd.tensor_scalar(J.nmr[:], J.mv[:, 0:1], -1.0, J.rstd[:], ALU.mult, ALU.mult
                                            ).then_inc(q["x_bias"], 1)
                if r == 2:
                    rsqrt(J.ve, J.ss[:], 1e-24, ALU.max, J.rinv, q["h_sq"], q["h_guard"], q["h_rinv"], t)
                if r == 3:
                    g = q["gate"]
                    pool.wait_ge(q["lg_repl"], t + 1)
                    nc.gpsimd.tensor_tensor(J.fb[:], J.R[:], J.L[:], ALU.subtract).then_inc(g, 1)
                    nc.gpsimd.tensor_scalar(J.na[:], J.v8[:, 0:1], 0.0, None, ALU.is_le).then_inc(g, 1)
                    nc.gpsimd.tensor_scalar(J.pos[:], J.L[:], 0.0, None, ALU.is_gt).then_inc(g, 1)
                    nc.gpsimd.tensor_scalar(J.RL[:], J.L[:], 0.0, None, ALU.max).then_inc(g, 1)
                    nc.gpsimd.tensor_scalar(J.nv[:], J.v8[:, 0:1], 0.0, -1.0, ALU.max, ALU.mult).then_inc(g, 1)
                    held(pool, (g, 7 * t + 5))
                    nc.gpsimd.tensor_scalar(J.fb2[:], J.fb[:], 0.0, J.na[:], ALU.is_lt, ALU.mult).then_inc(g, 1)
                    pool.wait_ge(g, 7 * t + 6)
                    nc.gpsimd.tensor_tensor(J.mk[:], J.fb2[:], J.pos[:], ALU.add).then_inc(g, 1)
                    pool.wait_ge(g, 7 * t + 7)
                    pool.wait_ge(q["gate_exp"], t + 1)
                    nc.gpsimd.tensor_tensor(J.em[:], J.eg[:], J.mk[:], ALU.mult).then_inc(q["gate_em"], 1)
                    pool.wait_ge(q["gate_sum"], t + 1)
                    pool.wait_ge(q["gate_sum"], t + 1)
                    nc.gpsimd.tensor_tensor(J.rgs[:], J.gs[:], minus_one[:], ALU.pow).then_inc(q["gate_rec"], 1)
                    held(pool, (q["gate_rec"], t + 1))
                    nc.gpsimd.tensor_scalar(J.rw[:], J.em[:], J.rgs[:], None, ALU.mult).then_inc(q["rw"], 1)
                if r in (5, 6, 7):
                    k = r - 4
                    pool.wait_ge(q["qkv_sc"], t * CHUNKS + 2 * k + 2)
                    if k > 1:
                        pool.wait_ge(q["qkv_add"], 4 * t + k - 1)
                    nc.gpsimd.tensor_tensor(J.MX[:, 0:4, :], J.MX[:, 0:4, :], J.MX[:, 4 * k:4 * k + 4, :], ALU.add
                                            ).then_inc(q["qkv_add"], 1)
                if r == 7:
                    pool.wait_ge(q["qkv_add"], 4 * t + 3)
                    nc.gpsimd.tensor_tensor(J.MX[:, 0:2, :], J.MX[:, 0:2, :], J.MX[:, 2:4, :], ALU.add
                                            ).then_inc(q["qkv_add"], 1)
                    pool.wait_ge(q["qkv_add"], 4 * t + 4)
                    nc.gpsimd.tensor_tensor(J.qk[:], J.MX[:, 0, 0:2 * ED], J.MX[:, 1, 0:2 * ED], ALU.add
                                            ).then_inc(q["qk_ready"], 1)
                    nc.gpsimd.tensor_tensor(J.vall[:, ds(t % TPB, 1), :].rearrange("p a d -> p (a d)"),
                                            J.MX[:, 0, 2 * ED:QKV], J.MX[:, 1, 2 * ED:QKV], ALU.add
                                            ).then_inc(q["v_ready"], 1)
                if r == 10:
                    held(pool, (q["sc_max"], t + 1))
                    nc.gpsimd.tensor_scalar(J.nm[:], J.mxr[:], -ED ** -0.5, None, ALU.mult).then_inc(q["sc_nmax"], 1)
                    pool.wait_ge(q["sc_exp"], t + 1)
                    nc.gpsimd.tensor_tensor(J.rrs[:], J.rs[:], minus_one[:], ALU.pow).then_inc(q["sc_rec"], 1)
                    held(pool, (q["sc_rec"], t + 1))
                    nc.gpsimd.tensor_scalar(J.rwn[:], J.rw[:], J.rrs[:], None, ALU.mult).then_inc(q["rw_sum"], 1)
                if r == 11:
                    pool.wait_ge(q["att_sb"], t + 1)
                    pool.wait_ge(q["rw_sum"], t + 1)
                    nc.gpsimd.tensor_tensor(J.mix[:], J.att[:].unsqueeze(1).broadcast_to([P, E, ED]),
                                            J.rwn[:].unsqueeze(2).broadcast_to([P, E, ED]), ALU.mult
                                            ).then_inc(q["mix"], 1)
                if J.n == "b" and r == 14:
                    rsqrt(vex, mvx[:, 1:2], 1e-5, ALU.add, rstdx, q["y_var"], q["y_eps"], q["y_rstd"], t)
                    held(pool, (q["y_rstd"], t + 1))
                    nc.gpsimd.tensor_scalar(nmrx[:], mvx[:, 0:1], -1.0, rstdx[:], ALU.mult, ALU.mult
                                            ).then_inc(q["y_bias"], 1)

            def step(pool, s, attn, prev, ta, tb, nx):
                for j in range(SLOTS):
                    u = lagged(s, j, OUT_LAG, attn, prev)
                    if u is not None:
                        lj = (j - OUT_LAG) % SLOTS
                        held(pool, (s_pr, u), (s_tk, u * PASSES + (2 * PASSES - 1 if lj % 2 == 0 else PASSES)))
                        at = 8 * (ROUNDS - 1) + LAST
                        nc.gpsimd.tensor_scalar(MK[:], S[:, lj % RING, :], M8[:, lj % RING, at:at + 1], None,
                                                ALU.is_ge).then_inc(s_ge, 1)
                        pool.wait_ge(s_ge, u + 1)
                        pool.wait_ge(s_ex, u + 1)
                        wait(pool, s_pt, u - 1)
                        nc.gpsimd.tensor_tensor(PR[:, lj % 2, :], MK[:], EX[:, lj % 2, :], ALU.mult
                                                ).then_inc(s_pr, 1)
                    u = lagged(s, j, EXP_LAG, attn, prev)
                    if u is not None:
                        lj = (j - EXP_LAG) % SLOTS
                        held(pool, (s_tk, u * PASSES + 1 if lj % 2 == 0 else u * PASSES - PASSES + 2))
                        nc.gpsimd.tensor_scalar(NM[:, lj % RING, :], M8[:, lj % RING, 0:1], -HD ** -0.5, None,
                                                ALU.mult).then_inc(s_nm, 1)
                    for J, t, r in both(ta, tb, j):
                        ffn(J, t, r)

            emit(pool, step)


def kernel(**inputs):
    import numpy as np
    import concourse.bacc as bacc
    from concourse.bass_utils import run_bass_kernel_spmd as run

    v = {k.replace("L0_", ""): np.ascontiguousarray(a) for k, a in inputs.items()}

    def heads(w):
        w = w.reshape(GROUPS, HG, HD, -1)
        w = np.concatenate([w, np.zeros_like(w)], axis=2)
        return w.reshape(GROUPS, P, -1)

    def by_chunk(w):
        return w.reshape(-1, P, w.shape[-1]).transpose(1, 0, 2)

    wq, wk = (heads(v[n]).transpose(0, 2, 1).reshape(GROUPS, KC, P, P) for n in ("attn_Wq", "attn_Wk"))
    arrays = {
        "x": v["attn_x"],
        "wqk": np.concatenate([wq, wk], axis=1).transpose(0, 2, 1, 3),
        "bqk": np.concatenate([heads(v["attn_bq"]), heads(v["attn_bk"])], axis=2),
        "wv": v["attn_Wv"].T.reshape(KC, P, GROUPS, HG * HD).transpose(2, 1, 0, 3),
        "bv": v["attn_bv"].reshape(GROUPS, HG * HD, 1),
        "wo": by_chunk(v["attn_Wo"].T),
        "bo": v["attn_bo"].reshape(1, D),
        "sim": v["ffn_sim_matrix"],
        "gates": v["ffn_gates"].reshape(1, E),
        "wf": by_chunk(np.concatenate([v["ffn_q_proj"], v["ffn_k_proj"], v["ffn_v_proj"]], axis=2)
                       .transpose(1, 0, 2).reshape(D, E * QKV)),
        "wof": by_chunk(v["ffn_o_proj"].reshape(E * ED, D)),
    }
    arrays = {k: np.ascontiguousarray(a) for k, a in arrays.items()}
    nc = bacc.Bacc("TRN2", target_bir_lowering=False, num_devices=1)
    args = [nc.dram_tensor(f"in_{k}", a.shape, mybir.dt.from_np(a.dtype), kind="ExternalInput").ap()
            for k, a in arrays.items()]
    out = nc.dram_tensor("out_y", (NB, T, D), F32, kind="ExternalOutput").ap()
    build(nc, *args, out)
    r = run(nc, [{f"in_{k}": a for k, a in arrays.items()}], core_ids=[0])
    return r.results[0]["out_y"]
```

```python
from contextlib import ExitStack

import concourse.bass as bass
from concourse import mybir

F32 = mybir.dt.float32
ALU = mybir.AluOpType
ACT = mybir.ActivationFunctionType
ds = bass.ds

P = 128
NB, T, D = 16, 512, 256
KC = D // P
TPB = T // P
TILES = NB * TPB
H, HD = 16, D // 16
HG = 4
GROUPS = H // HG
STEPS = NB * GROUPS
UNITS = HG * TPB
E, ED = 16, 64
QKV = 3 * ED
TOPK = 31
ROUNDS = (TOPK + 7) // 8
LAST = TOPK - 8 * (ROUNDS - 1) - 1
SLOTS = 16
V_SLOT, VT_SLOT = 5, 6
Q_SLOT, K_SLOT = 12, 13
RING = 8
TOP_LAG, EXP_LAG, MASK_LAG, OUT_LAG, EVAC_LAG, PV_LAG, CTX_LAG = 3, 4, 5, 6, 7, 7, 8
RINGE = 4
LAG_B = 5
LAG_A = 5
RINGX = 10
CHUNKS = E // 2
CTXW = HG * (HD + 1)
BIG = 3.0e38
MASKED = -1.0e30
START = {"a": 8, "b": 0}

BANK = {
    "ctxT": (-1, 2), "x": (0, 1), "hT": (2, 2), "lg": (3, 1), "ch0": (9, 1), "ch1": (9, 2), "ch2": (10, 1),
    "ch3": (10, 2), "ch4": (11, 1), "ch5": (12, 2), "ch6": (13, 1), "ch7": (13, 2), "qkT": (15, 1),
    "sc": (16, 1), "pT": (19, 2), "pv": (20, 2), "mixT0": (21, 1), "mixT1": (21, 2), "y": (22, 1),
    "xn": (25, 2),
}
ONLY_A, ONLY_B = ("ctxT", "x"), ("xn",)


AT = {
    "x_sum": (0, 1), "x_sq": (1, 1), "h": (2, 1), "gate_exp": (7, 1), "gate_sum": (8, 1), "sc_exp": (19, 1),
    "y_sq": (23, 1), "y_norm": (25, 1),
    "ctx_norm": -2, "x_mean": 0, "x_rstd": 1, "h_rinv": 2, "gate": 6, "gate_em": 7, "rw": 8, "add1": 11,
    "add2": 13, "add3": 14, "sc_mask": 16, "sc_nmax": 17, "rw_sum": 19, "mix": 20, "y_mean": 22, "y_rstd": 23,
    "ctx_rec": -2, "top": 5, "sc_max": 17,
}


def fill(job, key, t, last=False):
    keys = [k for k in BANK if k not in (ONLY_B if job == "a" else ONLY_A)]

    def time(k):
        return 2 * BANK[k][0] + BANK[k][1]

    own = keys.index(key)
    after = 0 if last else sum(time(k) + 2 * SLOTS < time(key) for k in keys)
    still = 0 if isinstance(t, int) and t == 0 else sum(time(k) - 2 * SLOTS > time(key) for k in keys)
    return t * len(keys) + (own + after - still)


def fills(job):
    return TILES * (len(BANK) - len(ONLY_B if job == "a" else ONLY_A))


def build(nc, x, wqk, bqk, wv, bv, wo, bo, sim, gates, wf, wof, out):
    with ExitStack() as ctx:
        def sb(name, *shape):
            return ctx.enter_context(nc.sbuf_tensor(name, list(shape), F32))

        def bank(name):
            return ctx.enter_context(nc.psum_tensor(name, [P, 512], F32))

        def sem(name):
            return ctx.enter_context(nc.semaphore(name))

        ident = sb("ident", P, P)
        ident2 = sb("ident2", P, P)
        ones = sb("ones", P, P)
        minus_half = sb("minus_half", P, E)
        minus_one = sb("minus_one", P, E)
        simg = sb("simg", P, E)
        maskw = sb("maskw", P, (2 * TPB - 1) * P)
        wo_sb = sb("wo_sb", P, KC, D)
        bo_row = sb("bo_row", 1, D)
        wf_sb = sb("wf_sb", P, KC, E * QKV)
        wof_sb = sb("wof_sb", P, E * ED // P, D)
        simn = sb("simn", P, KC, E)
        simsq = sb("simsq", P, KC, E)
        simr = sb("simr", P, E)
        gate_row = sb("gate_row", 1, 4, E)
        sig = sb("sig", P, E)

        wqk_cur = sb("wqk_cur", P, 2 * KC, P)
        bqk_cur = sb("bqk_cur", P, 2)
        wv_cur = sb("wv_cur", P, KC, HG * HD)
        bv_cur = sb("bv_cur", HG * HD, 1)
        xnT_all = sb("xnT_all", P, 2 * KC * T)
        xnT = sb("xnT", P, KC, T)
        QT = sb("QT", P, T)
        QTn = sb("QTn", P, T)
        KT = sb("KT", P, T)
        VT = sb("VT", HG * HD, T)
        V1 = sb("V1", P, TPB, HG, 2 * HD)
        cT = sb("cT", P, P)
        S = sb("S", P, RING, T)
        W = sb("W", P, 2, T)
        M8 = sb("M8", P, RING, 8 * ROUNDS)
        NM = sb("NM", P, RING, 1)
        MK = sb("MK", P, T)
        EX = sb("EX", P, RINGE, T)
        PTs = sb("PTs", P, 2, T)
        ctxr = sb("ctxr", P, 2, GROUPS, TPB * CTXW)
        x1r = sb("x1r", P, RINGX * D)
        crec = sb("crec", P, GROUPS, HG)
        ctxn = sb("ctxn", P, GROUPS, HG, HD)
        ctxT = sb("ctxT", P, KC, P)

        class Job:
            def __init__(self, n):
                self.n = n
                self.x = sb(f"x_{n}", P, 2 * D)
                self.sm = sb(f"sm_{n}", P, 1)
                self.mn = sb(f"mn_{n}", P, 1)
                self.vs = sb(f"vs_{n}", P, 1)
                self.Lr = sb(f"Lr_{n}", P, E)
                self.Sr = sb(f"Sr_{n}", P, T)
                self.ve = sb(f"ve_{n}", P, 1)
                self.rstd = sb(f"rstd_{n}", P, 1)
                self.h = sb(f"h_{n}", P, D)
                self.junk = sb(f"junk_{n}", P, D)
                self.ss = sb(f"ss_{n}", P, 1)
                self.nmr = sb(f"nmr_{n}", P, 1)
                self.rinv = sb(f"rinv_{n}", P, 1)
                self.hT = sb(f"hT_{n}", P, KC, P)
                self.L = sb(f"L_{n}", P, E)
                self.v8 = sb(f"v8_{n}", P, 8)
                self.mr8 = sb(f"mr8_{n}", P, 8)
                self.R = sb(f"R_{n}", P, E)
                self.fb = sb(f"fb_{n}", P, E)
                self.na = sb(f"na_{n}", P, 1)
                self.pos = sb(f"pos_{n}", P, E)
                self.fb2 = sb(f"fb2_{n}", P, E)
                self.mk = sb(f"mk_{n}", P, E)
                self.RL = sb(f"RL_{n}", P, E)
                self.nv = sb(f"nv_{n}", P, 1)
                self.eg = sb(f"eg_{n}", P, E)
                self.em = sb(f"em_{n}", P, E)
                self.gs = sb(f"gs_{n}", P, 1)
                self.rgs = sb(f"rgs_{n}", P, 1)
                self.rw = sb(f"rw_{n}", P, E)
                self.MX = sb(f"MX_{n}", P, E, QKV)
                self.qk = sb(f"qk_{n}", P, 2 * ED)
                self.vall = sb(f"vall_{n}", P, TPB, ED)
                self.qT = sb(f"qT_{n}", P, P)
                self.kT = sb(f"kT_{n}", P, T)
                self.mxr = sb(f"mxr_{n}", P, 1)
                self.nm = sb(f"nm_{n}", P, 1)
                self.Pf = sb(f"Pf_{n}", P, T)
                self.rs = sb(f"rs_{n}", P, 1)
                self.rrs = sb(f"rrs_{n}", P, 1)
                self.PTf = sb(f"PTf_{n}", P, T)
                self.rwn = sb(f"rwn_{n}", P, E)
                self.att = sb(f"att_{n}", P, ED)
                self.mix = sb(f"mix_{n}", P, E, ED)
                self.mixT = sb(f"mixT_{n}", P, E * ED // P, P)

        jobs = {n: Job(n) for n in "ab"}
        for n, J in jobs.items():
            J.F = bank(f"pF{n}")
            J.sem = {k: sem(f"{k}_{n}") for k in (
                "full", "read",
                "x_in", "x_sum", "x_mean", "x_sq", "x_eps", "x_rstd", "x_bias", "h_norm", "h_sq", "h_guard",
                "h_rinv", "lg", "lg_top", "lg_pair", "lg_repl", "gate", "gate_exp", "gate_em", "gate_sum",
                "gate_rec", "rw", "qkv_add", "qk_ready", "v_ready", "sc_mask", "sc_max", "sc_nmax", "sc_exp",
                "sc_rec", "rw_sum", "mix")}
        jobs["a"].sem.update({k: sem(k) for k in ("ctx_rec", "ctx_norm", "out_st")})
        jobs["b"].sem.update({k: sem(k) for k in ("y_mean", "y_sq", "y_eps", "y_rstd", "y_bias", "xn_norm")})
        y = sb("y", P, D)
        smy = sb("smy", P, 1)
        mny = sb("mny", P, 1)
        vsy = sb("vsy", P, 1)
        rstdx = sb("rstdx", P, 1)
        nmrx = sb("nmrx", P, 1)
        vex = sb("vex", P, 1)
        xn = sb("xn", P, D)

        pS = [bank("pS0"), bank("pS1")]
        pT = [bank("pT0"), bank("pT1")]
        pO = bank("pO")
        pG = bank("pG")

        s_ld = sem("s_ld")
        s_cst = sem("s_cst")
        s_passed = {e.engine: sem(f"s_passed_{n}") for n, e in (("pe", nc.tensor), ("dve", nc.vector),
                                                                ("pool", nc.gpsimd), ("act", nc.scalar))}
        s_ini = sem("s_ini")
        s_simsq, s_simps, s_simg, s_simr, s_simn = (sem("s_simsq"), sem("s_simps"), sem("s_simg"), sem("s_simr"),
                                                    sem("s_simn"))
        s_gexp, s_gadd, s_grec, s_gps, s_sig = (sem("s_gexp"), sem("s_gadd"), sem("s_grec"), sem("s_gps"),
                                                sem("s_sig"))
        s_w = sem("s_w")
        s_xc = sem("s_xc")
        s_qp, s_qe = sem("s_qp"), sem("s_qe")
        s_kp, s_ke = sem("s_kp"), sem("s_ke")
        s_vt, s_vte = sem("s_vt"), sem("s_vte")
        s_vp, s_ve = sem("s_vp"), sem("s_ve")
        s_sc = sem("s_sc")
        s_ev = sem("s_ev")
        s_tk = sem("s_tk")
        s_nm = sem("s_nm")
        s_ex = sem("s_ex")
        s_ge = sem("s_ge")
        s_pr = sem("s_pr")
        s_prd = sem("s_prd")
        s_pt = sem("s_pt")
        s_pe = sem("s_pe")
        s_pv = sem("s_pv")
        s_oc = sem("s_oc")
        s_ot = sem("s_ot")
        s_o = sem("s_o")
        PASSES = 2 * ROUNDS - 1
        TH = 8 * (ROUNDS - 1) + LAST

        block = ctx.enter_context(nc.Block())

        def wait(eng, s, v):
            if not isinstance(v, int) or v > 0:
                eng.wait_ge(s, v)

        def held(eng, *counts):
            for s, v in counts:
                wait(eng, s, v)
            eng.sem_inc(s_passed[eng.engine], 1)

        def emit(eng, step):
            none = (None, None)
            step(eng, None, False, False, none, (0, None), None)
            with eng.Fori(1, LAG_B - 1) as t:
                step(eng, None, False, False, none, (t, t - 1), None)
            step(eng, None, False, False, none, (LAG_B - 1, LAG_B - 2), 0)
            step(eng, 0, True, False, none, (LAG_B, LAG_B - 1), 1)
            with eng.Fori(1, LAG_A) as s:
                step(eng, s, True, True, none, (s + LAG_B, s + LAG_B - 1), s + 1)
            s = LAG_A
            step(eng, s, True, True, (0, None), (s + LAG_B, s + LAG_B - 1), s + 1)
            with eng.Fori(LAG_A + 1, STEPS - LAG_B) as s:
                step(eng, s, True, True, (s - LAG_A, s - LAG_A - 1), (s + LAG_B, s + LAG_B - 1), s + 1)
            s = STEPS - LAG_B
            step(eng, s, True, True, (s - LAG_A, s - LAG_A - 1), (None, TILES - 1), s + 1)
            with eng.Fori(STEPS - LAG_B + 1, STEPS) as s:
                step(eng, s, True, True, (s - LAG_A, s - LAG_A - 1), none, s + 1)
            step(eng, STEPS, False, True, (STEPS - LAG_A, STEPS - LAG_A - 1), none, None)
            with eng.Fori(STEPS + 1 - LAG_A, TILES) as t:
                step(eng, None, False, False, (t, t - 1), none, None)
            step(eng, None, False, False, (None, TILES - 1), none, None)

        def both(a, b, j):
            out = []
            for n, (t, before) in (("a", a), ("b", b)):
                if before is not None:
                    out.append((jobs[n], before, j - START[n] + SLOTS, t is None))
                if t is not None:
                    out.append((jobs[n], t, j - START[n], False))
            return out

        def masked(eng, s, l):
            if l < 0:
                s, l = s - 1, l + UNITS
            if isinstance(s, int) and s < 0:
                return
            if l % HG == HG - 1:
                wait(eng, s_prd, s * TPB + (l // HG + 1))
            else:
                wait(eng, s_pr, s * (UNITS - TPB) + (l // HG * (HG - 1) + l % HG + 1))

        def lagged(s, j, lag, attn, prev):
            if (j >= lag and not attn) or (j < lag and not prev):
                return None
            return s * UNITS + (j - lag)

        x_t = x.rearrange("b (n p) d -> (b n) p d", p=P)
        out_t = out.rearrange("b (n p) d -> (b n) p d", p=P)
        LOADS = 6

        @block.sync
        def _(sp):
            sp.dma_start(simn[:], sim.rearrange("(c p) e -> p c e", p=P)).then_inc(s_ld, 16)
            sp.dma_start(gate_row[:, 0, :], gates).then_inc(s_ld, 16)
            sp.dma_start(jobs["b"].x[:, 0:D], x_t[0]).then_inc(jobs["b"].sem["x_in"], 16)
            sp.dma_start(wf_sb[:], wf).then_inc(s_ld, 16)
            sp.dma_start(wof_sb[:], wof).then_inc(s_ld, 16)
            sp.dma_start(wo_sb[:], wo).then_inc(s_ld, 16)
            sp.dma_start(bo_row[:], bo).then_inc(s_ld, 16)

            def step(sp, s, attn, prev, a, b, nx):
                if nx is not None:
                    wait(sp, s_ke, nx)
                    wait(sp, s_vte, nx)
                    sp.dma_start(wqk_cur[:], wqk[ds(nx % GROUPS, 1)].rearrange("a p c m -> p (a c) m")
                                 ).then_inc(s_w, 16)
                    sp.dma_start(wv_cur[:], wv[ds(nx % GROUPS, 1)].rearrange("a p c m -> p (a c) m")
                                 ).then_inc(s_w, 16)
                    sp.dma_start(bv_cur[:], bv[ds(nx % GROUPS, 1)].rearrange("a p c -> p (a c)")
                                 ).then_inc(s_w, 16)
                    sp.dma_start(bqk_cur[:], bqk[ds(nx % GROUPS, 1)].rearrange("a p c -> p (a c)")
                                 ).then_inc(s_w, 16)
                    wait(sp, s_vt, nx)
                    nb = nx // GROUPS
                    last = isinstance(s, int) and s >= STEPS - LAG_B or (
                        s is not None and not isinstance(s, int) and s.min_val >= STEPS - LAG_B)
                    sp.wait_ge(jobs["b"].sem["read"],
                               fills("b") if last else fill("b", "xn", nb * TPB + TPB - 1) + 1)
                    sp.dma_start(xnT[:], xnT_all[:, ds((nb % 2) * KC * T, KC * T)]
                                 .rearrange("p (c t) -> p c t", c=KC)).then_inc(s_xc, 16)
                t, before = b
                if t is not None:
                    J = jobs["b"]
                    if before is not None:
                        sp.wait_ge(J.sem["full"], fill("b", "y", before) + 1)
                    sp.dma_start(J.x[:, ds((t + 1) % 2 * D, D)], x_t[ds((t + 1) % TILES, 1)]
                                 .rearrange("a p d -> (a p) d")).then_inc(J.sem["x_in"], 16)
                t, before = a
                if before is not None:
                    J = jobs["a"]
                    sp.wait_ge(J.sem["read"], fill("a", "y", before, t is None) + 1)
                    sp.dma_start(out_t[ds(before, 1)].rearrange("a p d -> (a p) d"), y[:]
                                 ).then_inc(J.sem["out_st"], 16)

            emit(sp, step)
            sp.wait_ge(jobs["a"].sem["out_st"], 16 * TILES)
            sp.wait_ge(jobs["b"].sem["x_in"], 16 * (TILES + 1))

        @block.tensor
        def _(pe):
            pe.wait_ge(s_ld, 16 * LOADS)
            pe.wait_ge(s_cst, 3)
            pe.wait_ge(s_simsq, 1)
            for c in range(KC):
                mm = nc.tensor.matmul(pG[:, 0:E], ones[:], simsq[:, c, :], start=c == 0, stop=c == KC - 1)
            mm.then_inc(s_simps, 1)
            pe.wait_ge(s_grec, 1)
            nc.tensor.matmul(pO[:, 0:E], ones[0:1, :], gate_row[:, 3, :], start=True, stop=True).then_inc(s_gps, 1)
            pe.wait_ge(s_simr, 1)
            pe.wait_ge(s_sig, 1)
            pe.wait_ge(s_simn, 1)
            pe.wait_ge(s_ini, 4)

            def x_add(F, two, src, t, ring):
                return nc.tensor.matmul(F[:, 0:D], (ident2 if two else ident)[:], src[:, ds((t % ring) * D, D)],
                                        start=False, stop=True)

            def ffn(J, t, r, part, last):
                q = J.sem
                F = J.F
                key = [k for k in BANK if BANK[k] == (r, part) and k not in (ONLY_B if J.n == "a" else ONLY_A)]
                if not key:
                    return
                key = key[0]
                ready = {"ctxT": ("ctx_norm", t + 1), "hT": ("h_norm", t + 1), "qkT": ("qk_ready", t + 1),
                         "pT": ("sc_exp", t + 1), "pv": ("v_ready", t + 1), "mixT0": ("mix", t + 1),
                         "xn": ("xn_norm", t + 1), "x": ("read", None), "y": ("read", None)}.get(key)
                waits = []
                if ready and ready[1] is not None:
                    waits.append((q[ready[0]], ready[1]))
                if key == "x":
                    waits.append((jobs["b"].sem["y_sq"], t + 1))
                waits.append((q["read"], fill(J.n, key, t, last)))
                if key == "qkT":
                    held(pe, *waits)
                else:
                    for w in waits:
                        wait(pe, *w)
                if key == "ctxT":
                    cn = ctxn[:].rearrange("p g h d -> p (g h d)")
                    for c in range(KC):
                        mm = nc.tensor.transpose(F[:, c * P:(c + 1) * P], cn[:, c * P:(c + 1) * P], ident[:])
                if key == "x":
                    for c in range(KC):
                        nc.tensor.matmul(F[:, 0:D], ctxT[:, c, :], wo_sb[:, c, :], start=c == 0, stop=False)
                    nc.tensor.matmul(F[:, 0:D], ones[0:1, :], bo_row[:], start=False, stop=False)
                    mm = x_add(F, False, x1r, t, RINGX)
                if key == "hT":
                    for c in range(KC):
                        mm = nc.tensor.transpose(F[:, c * P:(c + 1) * P], J.h[:, c * P:(c + 1) * P], ident[:])
                if key == "lg":
                    for c in range(KC):
                        mm = nc.tensor.matmul(F[:, 0:E], J.hT[:, c, :], simn[:, c, :], start=c == 0,
                                              stop=c == KC - 1)
                if key[:2] == "ch":
                    w = 2 * QKV
                    at = int(key[2:]) * w
                    for c in range(KC):
                        mm = nc.tensor.matmul(F[:, 0:w], J.hT[:, c, :], wf_sb[:, c, at:at + w],
                                              start=c == 0, stop=c == KC - 1)
                if key == "qkT":
                    for c in range(2):
                        mm = nc.tensor.transpose(F[0:ED, c * P:(c + 1) * P], J.qk[:, c * ED:(c + 1) * ED], ident[:])
                if key == "sc":
                    mm = nc.tensor.matmul(F[:, :], J.qT[0:ED, :], J.kT[0:ED, :], start=True, stop=True)
                if key == "pT":
                    for c in range(TPB):
                        mm = nc.tensor.transpose(F[:, c * P:(c + 1) * P], J.Pf[:, c * P:(c + 1) * P], ident[:])
                if key == "pv":
                    for c in range(TPB):
                        mm = nc.tensor.matmul(F[:, 0:ED], J.PTf[:, c * P:(c + 1) * P], J.vall[:, c, :],
                                              start=c == 0, stop=c == TPB - 1)
                if key[:4] == "mixT":
                    mx = J.mix[:].rearrange("p e d -> p (e d)")
                    for c in range(4):
                        k = 4 * int(key[4:]) + c
                        mm = nc.tensor.transpose(F[:, c * P:(c + 1) * P], mx[:, k * P:(k + 1) * P], ident[:])
                if key == "y":
                    for c in range(E * ED // P):
                        nc.tensor.matmul(F[:, 0:D], J.mixT[:, c, :], wof_sb[:, c, :], start=c == 0, stop=False)
                    mm = x_add(F, True, J.x, t, 2)
                if key == "xn":
                    for c in range(KC):
                        mm = nc.tensor.transpose(F[:, c * P:(c + 1) * P], xn[:, c * P:(c + 1) * P], ident[:])
                mm.then_inc(q["full"], 1)

            def step(pe, s, attn, prev, a, b, nx):
                for j in range(SLOTS):
                    qt, hh = divmod(j, HG)
                    if lagged(s, j, CTX_LAG, attn, prev) is not None and (j - CTX_LAG) % HG == HG - 1:
                        lq = (j - CTX_LAG) % SLOTS // HG
                        n = (s if j >= CTX_LAG else s - 1) * TPB + lq
                        pe.wait_ge(s_oc, n + 1)
                        nc.tensor.transpose(pO[:, P:2 * P], cT[:], ident[:]).then_inc(s_ot, 1)
                    if attn:
                        u = s * UNITS + j
                        if j == 0:
                            pe.wait_ge(s_ke, s + 1)
                        wait(pe, s_ev, u - 1)
                        r0 = 32 * hh
                        nc.tensor.matmul(pS[j % 2][:], QT[r0:r0 + HD, qt * P:(qt + 1) * P], KT[r0:r0 + HD, :],
                                         start=True, stop=True).then_inc(s_sc, 1)
                    for J, t, r, last in both(a, b, j):
                        ffn(J, t, r, 1, last)
                    u = lagged(s, j, OUT_LAG, attn, prev)
                    if u is not None:
                        lj = (j - OUT_LAG) % SLOTS
                        masked(pe, s, j - OUT_LAG)
                        wait(pe, s_pe, u - 1)
                        for c in range(TPB):
                            mm = nc.tensor.transpose(pT[lj % 2][:, c * P:(c + 1) * P],
                                                     EX[:, lj % RINGE, c * P:(c + 1) * P], ident[:])
                        mm.then_inc(s_pt, 1)
                    u = lagged(s, j, PV_LAG, attn, prev)
                    if u is not None:
                        lj = (j - PV_LAG) % SLOTS
                        lq, lh = divmod(lj, HG)
                        if lj == 0:
                            pe.wait_ge(s_ve, s + 1)
                        if lh == 0:
                            wait(pe, s_o, (s if j >= PV_LAG else s - 1) * TPB + lq)
                        pe.wait_ge(s_pe, u + 1)
                        for c in range(TPB):
                            mm = nc.tensor.matmul(pO[32 * lh:32 * lh + 32, 0:P], V1[:, c, lh, :],
                                                  PTs[:, lj % 2, c * P:(c + 1) * P],
                                                  start=c == 0, stop=c == TPB - 1)
                        mm.then_inc(s_pv, 1)
                    for J, t, r, last in both(a, b, j):
                        ffn(J, t, r, 2, last)
                    if attn and j == VT_SLOT:
                        held(pe, (s_vte, s + 1))
                        w = HG * HD
                        for n in range(TPB):
                            mm = nc.tensor.transpose(pG[:, n * w:(n + 1) * w], VT[:, n * P:(n + 1) * P],
                                                     ident[0:w, 0:w])
                        mm.then_inc(s_vp, 1)
                    if attn and j == V_SLOT:
                        pe.wait_ge(s_ke, s + 1)
                        for c in range(KC):
                            mm = nc.tensor.matmul(pG[0:HG * HD, :], wv_cur[:, c, :], xnT[:, c, :],
                                                  start=c == 0, stop=c == KC - 1)
                        mm.then_inc(s_vt, 1)
                    if nx is not None and j == Q_SLOT:
                        pe.wait_ge(s_w, 64 * (nx + 1))
                        pe.wait_ge(s_xc, 16 * (nx + 1))
                        if attn:
                            pe.wait_ge(s_ve, s + 1)
                        for c in range(KC):
                            mm = nc.tensor.matmul(pG[:, :], wqk_cur[:, c, :], xnT[:, c, :], start=c == 0,
                                                  stop=c == KC - 1)
                        mm.then_inc(s_qp, 1)
                    if nx is not None and j == K_SLOT:
                        pe.wait_ge(s_qe, nx + 1)
                        for c in range(KC):
                            mm = nc.tensor.matmul(pG[:, :], wqk_cur[:, KC + c, :], xnT[:, c, :], start=c == 0,
                                                  stop=c == KC - 1)
                        mm.then_inc(s_kp, 1)

            emit(pe, step)

        @block.scalar
        def _(act):
            act.wait_ge(s_ld, 16 * LOADS)
            nc.scalar.activation(gate_row[:, 1, :], gate_row[:, 0, :], ACT.Exp, scale=-1.0).then_inc(s_gexp, 1)
            act.wait_ge(s_gps, 1)
            nc.scalar.copy(sig[:], pO[:, 0:E]).then_inc(s_sig, 1)

            def ffn(J, t, r, part, last):
                q = J.sem
                F = J.F
                x_now = J.x[:, ds((t % 2) * D, D)]
                if J.n == "b" and (r, part) == AT["x_sum"]:
                    held(act, (q["x_in"], (t + 1) * 16))
                    nc.scalar.activation(J.junk[:], x_now, ACT.Copy, accum_out=J.sm[:]).then_inc(q["x_sum"], 1)
                if (r, part) == AT["x_sq"]:
                    held(act, (q["x_mean"], t + 1))
                    nc.scalar.activation(J.junk[:], x_now, ACT.Square, bias=J.mn[:], accum_out=J.vs[:]
                                         ).then_inc(q["x_sq"], 1)
                if (r, part) == AT["h"]:
                    held(act, (q["x_bias"], t + 1))
                    nc.scalar.activation(J.h[:], x_now, ACT.Identity, scale=J.rstd[:], bias=J.nmr[:]
                                         ).then_inc(q["h_norm"], 1)
                    act.wait_ge(q["h_norm"], t + 1)
                    nc.scalar.activation(J.junk[:], J.h[:], ACT.Square, accum_out=J.ss[:]).then_inc(q["h_sq"], 1)
                if (r, part) == AT["gate_exp"]:
                    act.wait_ge(q["gate"], 7 * t + 7)
                    nc.scalar.activation(J.eg[:], J.RL[:], ACT.Exp, bias=J.nv[:]).then_inc(q["gate_exp"], 1)
                if (r, part) == AT["gate_sum"]:
                    act.wait_ge(q["gate_em"], t + 1)
                    nc.scalar.activation(J.junk[:, 0:E], J.em[:], ACT.Copy, accum_out=J.gs[:]
                                         ).then_inc(q["gate_sum"], 1)
                if (r, part) == AT["sc_exp"]:
                    act.wait_ge(q["sc_nmax"], t + 1)
                    nc.scalar.activation(J.Pf[:], J.Sr[:], ACT.Exp, bias=J.nm[:], scale=ED ** -0.5,
                                         accum_out=J.rs[:]).then_inc(q["sc_exp"], 1)
                if J.n == "b" and (r, part) == AT["y_sq"]:
                    held(act, (q["y_mean"], t + 1))
                    nc.scalar.activation(J.junk[:], x1r[:, ds((t % RINGX) * D, D)], ACT.Square, bias=mny[:],
                                         accum_out=vsy[:]).then_inc(q["y_sq"], 1)
                if J.n == "b" and (r, part) == AT["y_norm"]:
                    held(act, (q["y_bias"], t + 1))
                    nc.scalar.activation(xn[:], x1r[:, ds((t % RINGX) * D, D)], ACT.Identity, scale=rstdx[:],
                                         bias=nmrx[:]).then_inc(q["xn_norm"], 1)
                key = [k for k in BANK if BANK[k] == (r, part) and k not in (ONLY_B if J.n == "a" else ONLY_A)]
                if not key:
                    return
                key = key[0]
                waits = [(q["full"], fill(J.n, key, t, last) + 1)]
                if key == "lg":
                    waits.append((q["h_rinv"], t + 1))
                if key == "ch0":
                    waits.append((q["rw"], t + 1))
                if key == "y" and J.n == "a":
                    waits.append((q["out_st"], t * 16))
                if key == "xn" and (not isinstance(t, int) and t.min_val >= LAG_B or isinstance(t, int) and
                                    t >= LAG_B):
                    waits.append((s_xc, (t - LAG_B + 1) * 16))
                held(act, *waits) if key in ("x", "y", "xn") else [wait(act, *w) for w in waits]
                two = F[:, 0:D].rearrange("p (c t) -> p c t", c=KC)
                if key == "ctxT":
                    ins = nc.scalar.copy(ctxT[:], two)
                if key == "x":
                    ins = nc.scalar.activation(x_now, F[:, 0:D], ACT.Copy, accum_out=J.sm[:])
                if key == "hT":
                    ins = nc.scalar.copy(J.hT[:], two)
                if key == "lg":
                    ins = nc.scalar.activation(J.Lr[:], F[:, 0:E], ACT.Copy, scale=J.rinv[:])
                if key[:2] == "ch":
                    for k in range(2):
                        e = 2 * int(key[2:]) + k
                        ins = nc.scalar.activation(J.MX[:, e, :], F[:, k * QKV:(k + 1) * QKV], ACT.Copy,
                                                   scale=J.rw[:, e:e + 1])
                if key == "qkT":
                    nc.scalar.copy(J.qT[0:ED, :], F[0:ED, 0:P])
                    ins = nc.scalar.copy(J.kT[0:ED, ds((t % TPB) * P, P)], F[0:ED, P:2 * P])
                if key == "sc":
                    ins = nc.scalar.copy(J.Sr[:], F[:])
                if key == "pT":
                    ins = nc.scalar.copy(J.PTf[:], F[:])
                if key == "pv":
                    ins = nc.scalar.copy(J.att[:], F[:, 0:ED])
                if key[:4] == "mixT":
                    k = 4 * int(key[4:])
                    ins = nc.scalar.copy(J.mixT[:, k:k + 4, :], F[:].rearrange("p (c t) -> p c t", c=4))
                if key == "y":
                    if J.n == "a":
                        ins = nc.scalar.activation(y[:], F[:, 0:D], ACT.Copy, scale=0.5)
                    else:
                        ins = nc.scalar.activation(x1r[:, ds((t % RINGX) * D, D)], F[:, 0:D], ACT.Copy,
                                                   scale=0.5, accum_out=smy[:])
                if key == "xn":
                    off = ((t // TPB) % 2) * (KC * T) + (t % TPB) * P
                    for c in range(KC):
                        ins = nc.scalar.copy(xnT_all[:, ds(off + c * T, P)], F[:, c * P:(c + 1) * P])
                ins.then_inc(q["read"], 1)

            def step(act, s, attn, prev, a, b, nx):
                for j in range(SLOTS):
                    u = lagged(s, j, EVAC_LAG, attn, prev)
                    if u is not None:
                        lj = (j - EVAC_LAG) % SLOTS
                        act.wait_ge(s_pt, u + 1)
                        wait(act, s_pv, u - 1)
                        nc.scalar.copy(PTs[:, lj % 2, :], pT[lj % 2][:]).then_inc(s_pe, 1)
                    u = lagged(s, j, EXP_LAG, attn, prev)
                    if u is not None:
                        lj = (j - EXP_LAG) % SLOTS
                        act.wait_ge(s_nm, (s if j >= EXP_LAG else s - 1) * (UNITS // 2) + (lj // 2 + 1))
                        wait(act, s_pt, u - (RINGE - 1))
                        nc.scalar.activation(EX[:, lj % RINGE, :], S[:, lj % RING, :], ACT.Exp,
                                             bias=NM[:, lj % RING, :], scale=HD ** -0.5).then_inc(s_ex, 1)
                    if attn:
                        u = s * UNITS + j
                        act.wait_ge(s_sc, u + 1)
                        masked(act, s, j - RING)
                        nc.scalar.copy(S[:, j % RING, :], pS[j % 2][:]).then_inc(s_ev, 1)
                    if lagged(s, j, CTX_LAG, attn, prev) is not None and (j - CTX_LAG) % HG == HG - 1:
                        lq = (j - CTX_LAG) % SLOTS // HG
                        ls = s if j >= CTX_LAG else s - 1
                        if not isinstance(ls, int) and ls.min_val >= LAG_A or isinstance(ls, int) and ls >= LAG_A:
                            act.wait_ge(jobs["a"].sem["ctx_norm"], ls - LAG_A + 1)
                        act.wait_ge(s_ot, ls * TPB + lq + 1)
                        nc.scalar.copy(ctxr[:, ds((ls // GROUPS) % 2, 1), ds(ls % GROUPS, 1),
                                            lq * CTXW:(lq + 1) * CTXW].rearrange("p a g (h e) -> p (a g h) e", h=HG),
                                       pO[:, P:2 * P].rearrange("p (h e) -> p h e", h=HG)[:, :, 0:HD + 1]
                                       ).then_inc(s_o, 1)
                    for J, t, r, last in both(a, b, j):
                        ffn(J, t, r, 1, last)
                    for J, t, r, last in both(a, b, j):
                        ffn(J, t, r, 2, last)
                    u = lagged(s, j, PV_LAG, attn, prev)
                    lj = (j - PV_LAG) % SLOTS
                    if u is not None and lj % HG == HG - 1:
                        n = (s if j >= PV_LAG else s - 1) * TPB + lj // HG
                        act.wait_ge(s_pv, u + 1)
                        nc.scalar.copy(cT[:], pO[:, 0:P]).then_inc(s_oc, 1)
                    if attn and j == V_SLOT:
                        act.wait_ge(s_vt, s + 1)
                        nc.scalar.activation(VT[:], pG[0:HG * HD, :], ACT.Identity, bias=bv_cur[:]).then_inc(s_vte, 1)
                    if attn and j == VT_SLOT:
                        act.wait_ge(s_vp, s + 1)
                        wait(act, s_pv, s * UNITS)
                        nc.scalar.copy(V1[:, :, :, 0:HD],
                                       pG[:, 0:D].rearrange("p (n h d) -> p n h d", n=TPB, h=HG)).then_inc(s_ve, 1)
                    if nx is not None and j == Q_SLOT:
                        act.wait_ge(s_qp, nx + 1)
                        nc.scalar.activation(QTn[:], pG[:], ACT.Identity, bias=bqk_cur[:, 0:1]).then_inc(s_qe, 1)
                    if nx is not None and j == 15:
                        if attn:
                            act.wait_ge(s_sc, (s + 1) * UNITS)
                        act.wait_ge(s_qe, nx + 1)
                        nc.scalar.copy(QT[:], QTn[:])
                        act.wait_ge(s_kp, nx + 1)
                        nc.scalar.activation(KT[:], pG[:], ACT.Identity, bias=bqk_cur[:, 1:2]).then_inc(s_ke, 1)

            emit(act, step)

        @block.vector
        def _(dve):
            nc.vector.memset(V1[:], 0.0).then_inc(s_ini, 1)
            dve.wait_ge(s_ini, 1)
            nc.vector.memset(V1[:, :, :, HD:HD + 1], 1.0)
            for n in "ab":
                J = jobs[n]
                nc.vector.memset(J.mr8[:], BIG)
                nc.vector.memset(J.kT[:], 0.0)
                ins = nc.vector.memset(J.vall[:], 0.0)
                ins.then_inc(s_ini, 1)
            dve.wait_ge(s_ld, 16 * LOADS)
            nc.vector.tensor_tensor(simsq[:], simn[:], simn[:], ALU.mult).then_inc(s_simsq, 1)
            dve.wait_ge(s_gexp, 1)
            nc.vector.tensor_scalar(gate_row[:, 2, :], gate_row[:, 1, :], 1.0, None, ALU.add).then_inc(s_gadd, 1)
            dve.wait_ge(s_gadd, 1)
            nc.vector.reciprocal(gate_row[:, 3, :], gate_row[:, 2, :]).then_inc(s_grec, 1)
            dve.wait_ge(s_simps, 1)
            nc.vector.tensor_scalar(simg[:], pG[:, 0:E], 1e-24, None, ALU.max).then_inc(s_simg, 1)
            dve.wait_ge(s_simr, 1)
            for c in range(KC):
                ins = nc.vector.tensor_tensor(simn[:, c, :], simn[:, c, :], simr[:], ALU.mult)
            ins.then_inc(s_simn, 1)
            dve.wait_ge(s_ini, 3)
            nc.vector.memset(M8[:], 0.0).then_inc(s_ini, 1)
            dve.wait_ge(s_ini, 4)
            dve.wait_ge(s_sig, 1)

            def ffn(J, t, r, last):
                q = J.sem
                if J.n == "a" and r == AT["ctx_rec"]:
                    held(dve, (s_o, (t // TPB) * (GROUPS * TPB) + GROUPS * TPB))
                    nc.vector.reciprocal(crec[:], ctxr[:, ds((t // TPB) % 2, 1), :, ds((t % TPB) * CTXW, CTXW)]
                                         .rearrange("p a g (h e) -> p (a g) h e", h=HG)[:, :, :, HD]
                                         ).then_inc(q["ctx_rec"], 1)
                if r == AT["top"]:
                    wait(dve, q["read"], fill(J.n, "lg", t, last) + 1)
                    nc.vector.tensor_tensor(J.L[:], J.Lr[:], sig[:], ALU.subtract).then_inc(q["lg"], 1)
                    held(dve, (q["lg"], t + 1))
                    nc.vector.max(J.v8[:], J.L[:]).then_inc(q["lg_top"], 1)
                    dve.wait_ge(q["lg_top"], t + 1)
                    nc.vector.tensor_copy(J.mr8[:, 0:2], J.v8[:, 0:2]).then_inc(q["lg_pair"], 1)
                    held(dve, (q["lg_pair"], t + 1))
                    nc.vector.match_replace(J.R[:], J.mr8[:], J.L[:], -BIG).then_inc(q["lg_repl"], 1)
                if r == AT["sc_max"]:
                    held(dve, (q["sc_mask"], t + 1))
                    nc.vector.reduce_max(J.mxr[:], J.Sr[:], axis=mybir.AxisListType.X).then_inc(q["sc_max"], 1)

            def keep(s, j, attn, prev):
                v = lagged(s, j, MASK_LAG + 1, attn, prev)
                l = (j - MASK_LAG - 1) % SLOTS
                if v is None or l % HG != HG - 1:
                    return
                dve.wait_ge(s_ex, v + 1)
                nc.vector.scalar_tensor_tensor(
                    out=EX[:, l % RINGE, :], in0=S[:, l % RING, :], scalar=M8[:, l % RING, TH:TH + 1],
                    in1=EX[:, l % RINGE, :], op0=ALU.is_ge, op1=ALU.mult).then_inc(s_prd, 1)

            def step(dve, s, attn, prev, a, b, nx):
                for j in range(SLOTS):
                    u = lagged(s, j, TOP_LAG, attn, prev)
                    if j % 2 == 1:
                        if u is None and prev and j < MASK_LAG + 1:
                            dve.wait_ge(s_tk, s * UNITS * PASSES)
                        keep(s, j, attn, prev)
                    if u is not None and j % 2 == 1:
                        done = u * PASSES
                        r0 = (j - TOP_LAG) % RING
                        src = [S[:, r0 + i, :] for i in range(2)]
                        for k in range(PASSES):
                            if k == 2:
                                dve.wait_ge(s_tk, done + 2)
                                nc.vector.tensor_scalar(NM[:, r0:r0 + 2, 0], M8[:, r0:r0 + 2, 0], -HD ** -0.5, None,
                                                        ALU.mult).then_inc(s_nm, 1)
                            for i in range(2):
                                m = M8[:, r0 + i, k // 2 * 8:k // 2 * 8 + 8]
                                if k == 0:
                                    held(dve, (s_ev, u + i + 1))
                                else:
                                    held(dve, (s_tk, done + 2 * k + i - 1))
                                if k % 2 == 0:
                                    nc.vector.max(m, src[i]).then_inc(s_tk, 1)
                                else:
                                    to = W[:, i, :]
                                    nc.vector.match_replace(to, m, src[i], -BIG).then_inc(s_tk, 1)
                                    src[i] = to
                    for J, t, r, last in both(a, b, j):
                        ffn(J, t, r, last)

            emit(dve, step)

        @block.gpsimd
        def _(pool):
            nc.gpsimd.memset(ident[:], 0.0).then_inc(s_cst, 1)
            nc.gpsimd.memset(ones[:], 1.0)
            nc.gpsimd.memset(minus_half[:], -0.5)
            nc.gpsimd.memset(minus_one[:], -1.0)
            nc.gpsimd.memset(maskw[:], 0.0).then_inc(s_cst, 1)
            pool.wait_ge(s_cst, 2)
            nc.gpsimd.affine_select(out=maskw[:], in_=maskw[:], compare_op=ALU.is_ge, fill=MASKED,
                                    base=(TPB - 1) * P, pattern=[[-1, (2 * TPB - 1) * P]], channel_multiplier=1)
            nc.gpsimd.affine_select(out=ident2[:], in_=ident[:], compare_op=ALU.not_equal, fill=2.0, base=0,
                                    pattern=[[-1, P]], channel_multiplier=1)
            nc.gpsimd.affine_select(out=ident[:], in_=ident[:], compare_op=ALU.not_equal, fill=1.0, base=0,
                                    pattern=[[-1, P]], channel_multiplier=1).then_inc(s_cst, 1)
            pool.wait_ge(s_cst, 3)
            pool.wait_ge(s_simg, 1)
            nc.gpsimd.tensor_tensor(simr[:], simg[:], minus_half[:], ALU.pow).then_inc(s_simr, 1)

            def rstd(src, v1, v2, op1, op2, guarded, out, src_ready, guard_ready, out_ready, t):
                held(pool, (src_ready, t + 1))
                ops = (op1,) if op2 is None else (op1, op2)
                nc.gpsimd.tensor_scalar(guarded[:], src[:], v1, v2, *ops).then_inc(guard_ready, 1)
                pool.wait_ge(guard_ready, t + 1)
                nc.gpsimd.tensor_tensor(out[:], guarded[:], minus_half[:, 0:1], ALU.pow).then_inc(out_ready, 1)

            def ffn(J, t, r, last):
                q = J.sem
                if J.n == "a" and r == AT["ctx_norm"]:
                    held(pool, (q["ctx_rec"], t + 1))
                    c = ctxr[:, ds((t // TPB) % 2, 1), :, ds((t % TPB) * CTXW, CTXW)].rearrange(
                        "p a g (h e) -> p (a g) h e", h=HG)
                    nc.gpsimd.tensor_tensor(ctxn[:], c[:, :, :, 0:HD],
                                            crec[:].unsqueeze(3).broadcast_to([P, GROUPS, HG, HD]),
                                            ALU.mult).then_inc(q["ctx_norm"], 1)
                if r == AT["x_mean"]:
                    held(pool, (q["x_sum"], t + 1) if J.n == "b" else (q["read"], fill("a", "x", t, last) + 1))
                    nc.gpsimd.tensor_scalar(J.mn[:], J.sm[:], -1.0 / D, None, ALU.mult).then_inc(q["x_mean"], 1)
                if r == AT["x_rstd"]:
                    rstd(J.vs, 1.0 / D, 1e-5, ALU.mult, ALU.add, J.ve, J.rstd, q["x_sq"], q["x_eps"],
                         q["x_rstd"], t)
                    held(pool, (q["x_rstd"], t + 1))
                    nc.gpsimd.tensor_scalar(J.nmr[:], J.mn[:], J.rstd[:], None, ALU.mult).then_inc(q["x_bias"], 1)
                if r == AT["h_rinv"]:
                    rstd(J.ss, 1e-24, None, ALU.max, None, J.ve, J.rinv, q["h_sq"], q["h_guard"], q["h_rinv"], t)
                if r == AT["gate"]:
                    g = q["gate"]
                    pool.wait_ge(q["lg_repl"], t + 1)
                    nc.gpsimd.tensor_tensor(J.fb[:], J.R[:], J.L[:], ALU.subtract).then_inc(g, 1)
                    nc.gpsimd.tensor_scalar(J.na[:], J.v8[:, 0:1], 0.0, None, ALU.is_le).then_inc(g, 1)
                    nc.gpsimd.tensor_scalar(J.pos[:], J.L[:], 0.0, None, ALU.is_gt).then_inc(g, 1)
                    nc.gpsimd.tensor_scalar(J.RL[:], J.L[:], 0.0, None, ALU.max).then_inc(g, 1)
                    nc.gpsimd.tensor_scalar(J.nv[:], J.v8[:, 0:1], 0.0, -1.0, ALU.max, ALU.mult).then_inc(g, 1)
                    held(pool, (g, 7 * t + 5))
                    nc.gpsimd.tensor_scalar(J.fb2[:], J.fb[:], 0.0, J.na[:], ALU.is_lt, ALU.mult).then_inc(g, 1)
                    pool.wait_ge(g, 7 * t + 6)
                    nc.gpsimd.tensor_tensor(J.mk[:], J.fb2[:], J.pos[:], ALU.add).then_inc(g, 1)
                if r == AT["gate_em"]:
                    pool.wait_ge(q["gate"], 7 * t + 7)
                    pool.wait_ge(q["gate_exp"], t + 1)
                    nc.gpsimd.tensor_tensor(J.em[:], J.eg[:], J.mk[:], ALU.mult).then_inc(q["gate_em"], 1)
                if r == AT["rw"]:
                    pool.wait_ge(q["gate_sum"], t + 1)
                    nc.gpsimd.tensor_tensor(J.rgs[:], J.gs[:], minus_one[:, 0:1], ALU.pow).then_inc(q["gate_rec"], 1)
                    held(pool, (q["gate_rec"], t + 1))
                    nc.gpsimd.tensor_scalar(J.rw[:], J.em[:], J.rgs[:], None, ALU.mult).then_inc(q["rw"], 1)
                for k in (1, 2, 3):
                    if r != AT[f"add{k}"]:
                        continue
                    pool.wait_ge(q["read"], fill(J.n, f"ch{2 * k + 1}", t, last) + 1)
                    if k > 1:
                        pool.wait_ge(q["qkv_add"], 4 * t + k - 1)
                    nc.gpsimd.tensor_tensor(J.MX[:, 0:4, :], J.MX[:, 0:4, :], J.MX[:, 4 * k:4 * k + 4, :], ALU.add
                                            ).then_inc(q["qkv_add"], 1)
                if r == AT["add3"]:
                    pool.wait_ge(q["qkv_add"], 4 * t + 3)
                    nc.gpsimd.tensor_tensor(J.MX[:, 0:2, :], J.MX[:, 0:2, :], J.MX[:, 2:4, :], ALU.add
                                            ).then_inc(q["qkv_add"], 1)
                    pool.wait_ge(q["qkv_add"], 4 * t + 4)
                    nc.gpsimd.tensor_tensor(J.qk[:], J.MX[:, 0, 0:2 * ED], J.MX[:, 1, 0:2 * ED], ALU.add
                                            ).then_inc(q["qk_ready"], 1)
                    nc.gpsimd.tensor_tensor(J.vall[:, ds(t % TPB, 1), :].rearrange("p a d -> p (a d)"),
                                            J.MX[:, 0, 2 * ED:QKV], J.MX[:, 1, 2 * ED:QKV], ALU.add
                                            ).then_inc(q["v_ready"], 1)
                if r == AT["sc_mask"]:
                    held(pool, (q["read"], fill(J.n, "sc", t, last) + 1))
                    nc.gpsimd.tensor_tensor(J.Sr[:], J.Sr[:], maskw[:, ds((TPB - 1 - t % TPB) * P, T)], ALU.add
                                            ).then_inc(q["sc_mask"], 1)
                if r == AT["sc_nmax"]:
                    held(pool, (q["sc_max"], t + 1))
                    nc.gpsimd.tensor_scalar(J.nm[:], J.mxr[:], -ED ** -0.5, None, ALU.mult).then_inc(q["sc_nmax"], 1)
                if r == AT["rw_sum"]:
                    pool.wait_ge(q["sc_exp"], t + 1)
                    nc.gpsimd.tensor_tensor(J.rrs[:], J.rs[:], minus_one[:, 0:1], ALU.pow).then_inc(q["sc_rec"], 1)
                    held(pool, (q["sc_rec"], t + 1))
                    nc.gpsimd.tensor_scalar(J.rwn[:], J.rw[:], J.rrs[:], None, ALU.mult).then_inc(q["rw_sum"], 1)
                if r == AT["mix"]:
                    pool.wait_ge(q["read"], fill(J.n, "pv", t, last) + 1)
                    pool.wait_ge(q["rw_sum"], t + 1)
                    nc.gpsimd.tensor_tensor(J.mix[:], J.att[:].unsqueeze(1).broadcast_to([P, E, ED]),
                                            J.rwn[:].unsqueeze(2).broadcast_to([P, E, ED]), ALU.mult
                                            ).then_inc(q["mix"], 1)
                if J.n == "b" and r == AT["y_mean"]:
                    held(pool, (q["read"], fill("b", "y", t, last) + 1))
                    nc.gpsimd.tensor_scalar(mny[:], smy[:], -1.0 / D, None, ALU.mult).then_inc(q["y_mean"], 1)
                if J.n == "b" and r == AT["y_rstd"]:
                    rstd(vsy, 1.0 / D, 1e-5, ALU.mult, ALU.add, vex, rstdx, q["y_sq"], q["y_eps"], q["y_rstd"], t)
                    held(pool, (q["y_rstd"], t + 1))
                    nc.gpsimd.tensor_scalar(nmrx[:], mny[:], rstdx[:], None, ALU.mult).then_inc(q["y_bias"], 1)

            def step(pool, s, attn, prev, a, b, nx):
                for j in range(SLOTS):
                    u = lagged(s, j, MASK_LAG, attn, prev)
                    lj = (j - MASK_LAG) % SLOTS
                    if u is not None and lj % HG < HG - 1:
                        n = (s if j >= MASK_LAG else s - 1) * (UNITS - TPB) + (lj // HG * (HG - 1) + lj % HG)
                        held(pool, (s_pr, n), (s_tk, u * PASSES + (2 * PASSES - 1 if lj % 2 == 0 else PASSES)))
                        nc.gpsimd.tensor_scalar(MK[:], S[:, lj % RING, :], M8[:, lj % RING, TH:TH + 1], None,
                                                ALU.is_ge).then_inc(s_ge, 1)
                        pool.wait_ge(s_ge, n + 1)
                        pool.wait_ge(s_ex, u + 1)
                        nc.gpsimd.tensor_tensor(EX[:, lj % RINGE, :], MK[:], EX[:, lj % RINGE, :], ALU.mult
                                                ).then_inc(s_pr, 1)
                    for J, t, r, last in both(a, b, j):
                        ffn(J, t, r, last)

            emit(pool, step)


def kernel(**inputs):
    import numpy as np
    import concourse.bacc as bacc
    from concourse.bass_utils import run_bass_kernel_spmd as run

    v = {k.replace("L0_", ""): np.ascontiguousarray(a) for k, a in inputs.items()}

    def heads(w):
        w = w.reshape(GROUPS, HG, HD, -1)
        w = np.concatenate([w, np.zeros_like(w)], axis=2)
        return w.reshape(GROUPS, P, -1)

    def by_chunk(w):
        return w.reshape(-1, P, w.shape[-1]).transpose(1, 0, 2)

    wq, wk = (heads(v[n]).transpose(0, 2, 1).reshape(GROUPS, KC, P, P) for n in ("attn_Wq", "attn_Wk"))
    arrays = {
        "x": v["attn_x"],
        "wqk": np.concatenate([wq, wk], axis=1).transpose(0, 2, 1, 3),
        "bqk": np.concatenate([heads(v["attn_bq"]), heads(v["attn_bk"])], axis=2),
        "wv": v["attn_Wv"].T.reshape(KC, P, GROUPS, HG * HD).transpose(2, 1, 0, 3),
        "bv": v["attn_bv"].reshape(GROUPS, HG * HD, 1),
        "wo": by_chunk(v["attn_Wo"].T),
        "bo": v["attn_bo"].reshape(1, D),
        "sim": v["ffn_sim_matrix"],
        "gates": v["ffn_gates"].reshape(1, E),
        "wf": by_chunk(np.concatenate([v["ffn_q_proj"], v["ffn_k_proj"], v["ffn_v_proj"]], axis=2)
                       .transpose(1, 0, 2).reshape(D, E * QKV)),
        "wof": by_chunk(v["ffn_o_proj"].reshape(E * ED, D)),
    }
    arrays = {k: np.ascontiguousarray(a) for k, a in arrays.items()}
    nc = bacc.Bacc("TRN2", target_bir_lowering=False, num_devices=1)
    args = [nc.dram_tensor(f"in_{k}", a.shape, mybir.dt.from_np(a.dtype), kind="ExternalInput").ap()
            for k, a in arrays.items()]
    out = nc.dram_tensor("out_y", (NB, T, D), F32, kind="ExternalOutput").ap()
    build(nc, *args, out)
    r = run(nc, [{f"in_{k}": a for k, a in arrays.items()}], core_ids=[0])
    return r.results[0]["out_y"]
```
